# Optimizing a Trainium2 kernel written in Bass

```python
import numpy as np
import jax
import jax.numpy as jnp

def _softmax(x, axis=-1):
    return jax.nn.softmax(x, axis=axis)
def _gelu(x):
    return jax.nn.gelu(x, approximate=True)
def _silu(x):
    return jax.nn.silu(x)
def _sigmoid(x):
    return jax.nn.sigmoid(x)
def _layernorm(x, axis=-1, eps=1e-5):
    m = jnp.mean(x, axis=axis, keepdims=True)
    v = jnp.var(x, axis=axis, keepdims=True)
    return (x - m) / jnp.sqrt(v + eps)
def _scatter_add(tgt, idx, src, axis=0):
    return tgt.at[idx].add(src)
def _segment_sum(src, seg, n):
    return jax.ops.segment_sum(src, seg, n)

kernel_name = 'mk_adj_resnorm_d4_adj_256_89f9fb'

def setup_inputs(seed: int = 0):
    np.random.seed(seed)
    _w = jnp.asarray
    def _rec_inputs():
        import jax
        import jax.numpy as jnp
        _gk = jax.random.key(seed)
        x = -0.0002928 + 1 * jax.random.normal(jax.random.fold_in(_gk, 1), (16, 1024, 256), jnp.float32)
        _w = (1.0 + jnp.arange(1024, dtype=jnp.float32)) ** -0.5
        _w = _w / _w.mean()
        _pij = jnp.clip(0.015625 * _w[:, None] * _w[None, :], 0.0, 1.0)
        _a = jax.random.uniform(jax.random.fold_in(_gk, 2), (16, 1024, 1024)) < _pij
        _a = jnp.logical_or(_a, jnp.swapaxes(_a, -1, -2))
        _a = jnp.logical_or(_a, jnp.eye(1024, dtype=bool))
        _af = _a.astype(jnp.float32)
        _af = _af * jax.random.uniform(jax.random.fold_in(_gk, 3), (16, 1024, 1024), jnp.float32, 0.05, 4.42607)
        adj = _af
        return x, adj
    x, adj = _rec_inputs()
    def _L0_gnn_setup():
        import math
        import jax, jax.numpy as jnp
        import numpy as np
        B, N, D, H = (32, 512, 256, 8)
        HD = D // H
        key = jax.random.key(seed)
        ks = jax.random.split(key, 9)
        h = jax.random.normal(ks[0], (B, N, D), dtype=jnp.float32)
        edge = jax.random.normal(ks[1], (B, N, N), dtype=jnp.float32)
        adj = jax.random.uniform(ks[2], (B, N, N)) < 0.5
        adj_mask = adj | jnp.eye(N, dtype=bool)[None]
        s = 1.0 / math.sqrt(D)
        W_q = jax.random.normal(ks[3], (D, D), dtype=jnp.float32) * s
        W_k = jax.random.normal(ks[4], (D, D), dtype=jnp.float32) * s
        W_v = jax.random.normal(ks[5], (D, D), dtype=jnp.float32) * s
        W_e = jax.random.normal(ks[6], (H, 1), dtype=jnp.float32)
        W_o = jax.random.normal(ks[7], (D, D), dtype=jnp.float32) * s
        return {'h': h, 'edge': edge, 'adj_mask': adj_mask, 'W_q': W_q, 'W_k': W_k, 'W_v': W_v, 'W_e': W_e, 'W_o': W_o}
    _L0_gnn_all = _L0_gnn_setup()
    _L0_gnn_in = {k: v for k, v in _L0_gnn_all.items() if k in ('W_q', 'W_k', 'W_v', 'W_e', 'W_o', )}
    del _L0_gnn_all

    def _L1_gnn_setup():
        import jax, jax.numpy as jnp
        import numpy as np
        LN_EPS = 1e-05
        key = jax.random.key(seed)
        k1, k2, k3, k4 = jax.random.split(key, 4)
        B, N, F, O = (8, 2048, 256, 256)
        x = jax.random.normal(k1, (B, N, F), dtype=jnp.float32)
        adj = jax.random.uniform(k2, (B, N, N), dtype=jnp.float32)
        gamma = jnp.ones((F,), jnp.float32)
        beta = jnp.zeros((F,), jnp.float32)
        W_self = jax.random.normal(k3, (F, O), dtype=jnp.float32) * (1.0 / np.sqrt(F))
        W_neigh = jax.random.normal(k4, (F, O), dtype=jnp.float32) * (1.0 / np.sqrt(F))
        return {'x': x, 'adj': adj, 'gamma': gamma, 'beta': beta, 'W_self': W_self, 'W_neigh': W_neigh}
    _L1_gnn_all = _L1_gnn_setup()
    _L1_gnn_in = {k: v for k, v in _L1_gnn_all.items() if k in ('gamma', 'beta', 'W_self', 'W_neigh', )}
    del _L1_gnn_all

    def _L2_gnn_setup():
        import jax, jax.numpy as jnp
        import numpy as np
        B, K, H = (32, 1024, 256)
        LN_EPS = 1e-05

        def layer_norm(x, gamma, beta):
            mu = jnp.mean(x, axis=-1, keepdims=True)
            var = jnp.mean(jnp.square(x - mu), axis=-1, keepdims=True)
            return (x - mu) * jax.lax.rsqrt(var + LN_EPS) * gamma + beta
        key = jax.random.key(seed)
        k1, k2, k3, k4 = jax.random.split(key, 4)
        x = jax.random.normal(k1, (B, K, H), dtype=jnp.float32)
        adj = jax.random.uniform(k2, (B, K, K), dtype=jnp.float32)
        s = 1.0 / np.sqrt(H)
        W_rel = jax.random.normal(k3, (H, H), dtype=jnp.float32) * s
        b_rel = jnp.zeros((H,), dtype=jnp.float32)
        W_root = jax.random.normal(k4, (H, H), dtype=jnp.float32) * s
        ln_gamma = jnp.ones((H,), dtype=jnp.float32)
        ln_beta = jnp.zeros((H,), dtype=jnp.float32)
        return {'x': x, 'adj': adj, 'W_rel': W_rel, 'b_rel': b_rel, 'W_root': W_root, 'ln_gamma': ln_gamma, 'ln_beta': ln_beta}
    _L2_gnn_all = _L2_gnn_setup()
    _L2_gnn_in = {k: v for k, v in _L2_gnn_all.items() if k in ('W_rel', 'b_rel', 'W_root', 'ln_gamma', 'ln_beta', )}
    del _L2_gnn_all

    def _L3_gnn_setup():
        import jax, jax.numpy as jnp
        import numpy as np
        D_IN = 256
        D_HID = 512
        key = jax.random.key(seed)
        k1, k2, k3, k4, k5, k6 = jax.random.split(key, 6)
        x = jax.random.normal(k1, (8, 4096, D_IN), dtype=jnp.float32)
        adj = jax.random.uniform(k2, (8, 4096, 4096), dtype=jnp.float32)
        s1 = 1.0 / np.sqrt(D_IN)
        s2 = 1.0 / np.sqrt(D_HID)
        W1 = jax.random.uniform(k3, (D_IN, D_HID), dtype=jnp.float32, minval=-s1, maxval=s1)
        b1 = jax.random.uniform(k4, (D_HID,), dtype=jnp.float32, minval=-s1, maxval=s1)
        W2 = jax.random.uniform(k5, (D_HID, D_IN), dtype=jnp.float32, minval=-s2, maxval=s2)
        b2 = jax.random.uniform(k6, (D_IN,), dtype=jnp.float32, minval=-s2, maxval=s2)
        eps = jnp.zeros((1,), dtype=jnp.float32)
        return {'x': x, 'adj': adj, 'eps': eps, 'W1': W1, 'b1': b1, 'W2': W2, 'b2': b2}
    _L3_gnn_all = _L3_gnn_setup()
    _L3_gnn_in = {k: v for k, v in _L3_gnn_all.items() if k in ('eps', 'W1', 'b1', 'W2', 'b2', )}
    del _L3_gnn_all

    return {
        "x": x,
        "adj": adj,
        "L0_gnn_W_q": _L0_gnn_in["W_q"],
        "L0_gnn_W_k": _L0_gnn_in["W_k"],
        "L0_gnn_W_v": _L0_gnn_in["W_v"],
        "L0_gnn_W_e": _L0_gnn_in["W_e"],
        "L0_gnn_W_o": _L0_gnn_in["W_o"],
        "L1_gnn_gamma": _L1_gnn_in["gamma"],
        "L1_gnn_beta": _L1_gnn_in["beta"],
        "L1_gnn_W_self": _L1_gnn_in["W_self"],
        "L1_gnn_W_neigh": _L1_gnn_in["W_neigh"],
        "L2_gnn_W_rel": _L2_gnn_in["W_rel"],
        "L2_gnn_b_rel": _L2_gnn_in["b_rel"],
        "L2_gnn_W_root": _L2_gnn_in["W_root"],
        "L2_gnn_ln_gamma": _L2_gnn_in["ln_gamma"],
        "L2_gnn_ln_beta": _L2_gnn_in["ln_beta"],
        "L3_gnn_eps": _L3_gnn_in["eps"],
        "L3_gnn_W1": _L3_gnn_in["W1"],
        "L3_gnn_b1": _L3_gnn_in["b1"],
        "L3_gnn_W2": _L3_gnn_in["W2"],
        "L3_gnn_b2": _L3_gnn_in["b2"],
    }

def reference(x, adj, L0_gnn_W_q, L0_gnn_W_k, L0_gnn_W_v, L0_gnn_W_e, L0_gnn_W_o, L1_gnn_gamma, L1_gnn_beta, L1_gnn_W_self, L1_gnn_W_neigh, L2_gnn_W_rel, L2_gnn_b_rel, L2_gnn_W_root, L2_gnn_ln_gamma, L2_gnn_ln_beta, L3_gnn_eps, L3_gnn_W1, L3_gnn_b1, L3_gnn_W2, L3_gnn_b2):
    import jax
    import jax.numpy as jnp
    def _L0_gnn_ref(h, edge, adj_mask, W_q, W_k, W_v, W_e, W_o):
        import math
        import jax, jax.numpy as jnp
        import numpy as np
        B, N, D, H = (32, 512, 256, 8)
        HD = D // H
        b, n, _ = h.shape
        q = (h @ W_q.T).reshape(b, n, H, HD).transpose(0, 2, 1, 3)
        k = (h @ W_k.T).reshape(b, n, H, HD).transpose(0, 2, 1, 3)
        v = (h @ W_v.T).reshape(b, n, H, HD).transpose(0, 2, 1, 3)
        edge_bias = jnp.einsum('bij,h->bhij', edge, W_e[:, 0])
        scores = jnp.einsum('bhid,bhjd->bhij', q, k) / math.sqrt(HD) + edge_bias
        scores = jnp.where(adj_mask[:, None], scores, -jnp.inf)
        attn = jax.nn.softmax(scores, axis=-1)
        out = jnp.einsum('bhij,bhjd->bhid', attn, v)
        out = out.transpose(0, 2, 1, 3).reshape(b, n, D)
        return out @ W_o.T

    def _L1_gnn_ref(x, adj, gamma, beta, W_self, W_neigh):
        import jax, jax.numpy as jnp
        import numpy as np
        LN_EPS = 1e-05
        mu = jnp.mean(x, axis=-1, keepdims=True)
        var = jnp.mean(jnp.square(x - mu), axis=-1, keepdims=True)
        xn = (x - mu) * jax.lax.rsqrt(var + LN_EPS) * gamma + beta
        d_out = jnp.sum(adj, axis=1)
        d_in = jnp.sum(adj, axis=2)
        s_out = jnp.where(d_out != 0, jax.lax.rsqrt(d_out), 0.0)
        s_in = jnp.where(d_in != 0, jax.lax.rsqrt(d_in), 0.0)
        A_norm = s_out[:, :, None] * adj * s_in[:, None, :]
        eye = jnp.eye(adj.shape[1], dtype=adj.dtype)
        L = eye[None, :, :] - A_norm
        neighbor = jnp.einsum('bij,bjf->bif', L, xn)
        pre = xn @ W_self + neighbor @ W_neigh
        return jax.nn.softplus(pre)

    def _L2_gnn_ref(x, adj, W_rel, b_rel, W_root, ln_gamma, ln_beta):
        import jax, jax.numpy as jnp
        import numpy as np
        B, K, H = (32, 1024, 256)
        LN_EPS = 1e-05

        def layer_norm(x, gamma, beta):
            mu = jnp.mean(x, axis=-1, keepdims=True)
            var = jnp.mean(jnp.square(x - mu), axis=-1, keepdims=True)
            return (x - mu) * jax.lax.rsqrt(var + LN_EPS) * gamma + beta
        h = layer_norm(x, ln_gamma, ln_beta)
        agg = jnp.einsum('bij,bjh->bih', adj, h)
        conv = jnp.einsum('bkh,ho->bko', agg, W_rel) + b_rel + jnp.einsum('bkh,ho->bko', h, W_root)
        return x + jax.nn.relu(conv)

    def _L3_gnn_ref(x, adj, eps, W1, b1, W2, b2):
        import jax, jax.numpy as jnp
        import numpy as np
        D_IN = 256
        D_HID = 512
        aggregated = jnp.einsum('bnm,bmd->bnd', adj, x)
        h = (1.0 + eps) * x + aggregated
        h = jax.nn.relu(h @ W1 + b1)
        return h @ W2 + b2

    x = _layernorm(x + _L0_gnn_ref(x, adj, adj, L0_gnn_W_q, L0_gnn_W_k, L0_gnn_W_v, L0_gnn_W_e, L0_gnn_W_o), axis=-1)
    x = _layernorm(x + _L1_gnn_ref(x, adj, L1_gnn_gamma, L1_gnn_beta, L1_gnn_W_self, L1_gnn_W_neigh), axis=-1)
    x = _layernorm(x + _L2_gnn_ref(x, adj, L2_gnn_W_rel, L2_gnn_b_rel, L2_gnn_W_root, L2_gnn_ln_gamma, L2_gnn_ln_beta), axis=-1)
    x = _layernorm(x + _L3_gnn_ref(x, adj, L3_gnn_eps, L3_gnn_W1, L3_gnn_b1, L3_gnn_W2, L3_gnn_b2), axis=-1)
    return x


_drawn_inputs = setup_inputs


def setup_inputs(seed=0):
    import zlib

    import numpy as np

    out = dict(_drawn_inputs(seed))
    spreads = {'L1_gnn_gamma': (1.0, 0.2),
     'L1_gnn_beta': (0.0, 0.1),
     'L2_gnn_b_rel': (0.0, 0.8),
     'L2_gnn_ln_gamma': (1.0, 0.2),
     'L2_gnn_ln_beta': (0.0, 0.1)}
    factors = {'L3_gnn_b1': 26.389, 'L3_gnn_b2': 8.0}
    for name, (base, spread) in spreads.items():
        noise = np.random.default_rng([zlib.crc32(name.encode()), seed]).standard_normal(out[name].shape)
        drawn = base * np.exp(spread * noise) if base else spread * noise
        out[name] = jnp.asarray(drawn.astype(out[name].dtype))
    for name, factor in factors.items():
        out[name] = (out[name] * factor).astype(out[name].dtype)
    return out
```

```python
from contextlib import ExitStack

import concourse.bass as bass
from concourse import mybir

F32 = mybir.dt.float32
F32R = mybir.dt.float32r
BF16 = mybir.dt.bfloat16
ALU = mybir.AluOpType
ACT = mybir.ActivationFunctionType
AX = mybir.AxisListType

P = 128
LN_EPS = 1e-5
MASKED = -1e30
KB = 1024


class Tally:

    def __init__(self, sem, per_batch, base=0):
        self.sem, self.per_batch, self.base = sem, per_batch, base

    def at(self, b, count):
        return b * self.per_batch + (self.base + count)


def gnn_stack_kernel(nc: bass.Bass, x, adj, W_qT, W_kT, W_vT, W_e, W_oT, L1_gamma, L1_beta, L1_W_self, L1_W_neigh,
                     L2_W_rel, L2_b_rel, L2_W_root, L2_gamma, L2_beta, L3_eps, L3_W1, L3_b1, L3_W2, L3_b2, out):
    B, N, D = x.shape
    H = W_e.shape[0]
    HD = D // H
    HID = L3_W1.shape[1]
    NT = N // P
    CT = D // P
    KT = HID // P
    HALF = 512
    NH = N // HALF
    TPH = HALF // P
    NP = NT // 2
    G = P // HD
    HG = H // G
    UNITS = NT * H
    GROUPS = UNITS // G
    PT_SLOTS = 6
    SCALE = float(HD) ** -0.5
    assert 2 * D == HALF and G * HD == P and 4 * HD == P

    x_t = x.rearrange("b (t p) d -> b p t d", p=P)
    out_t = out.rearrange("b (t p) d -> b p t d", p=P)
    adj_t = adj.rearrange("b (t p) j -> b p t j", p=P)

    ctx = ExitStack()
    with ctx:
        place = [(nc.sbuf_base + 63) // 64 * 64]

        def at(name, offset, shape, dt):
            return nc.alloc_sbuf_tensor_at(name, shape, dt, offset=offset).ap()

        def sb(name, shape, dt=F32):
            size = 2 if dt == BF16 else 4
            for n in shape[1:]:
                size *= n
            offset = place[0]
            place[0] += (size + 63) // 64 * 64
            return at(name, offset, shape, dt)

        wq = sb("wq", [P, CT, D])
        wk = sb("wk", [P, CT, D])
        wv = sb("wv", [P, CT, D])
        wo = sb("wo", [P, CT, D])
        w_ns = sb("w_ns", [P, CT, 2, D])
        w_rel = sb("w_rel", [P, CT, D])
        w_root = sb("w_root", [P, CT, D])
        w1 = sb("w1", [P, CT, HID])
        w2 = sb("w2", [P, KT, D])
        brel_bc = sb("brel_bc", [P, D])
        b2_bc = sb("b2_bc", [P, D])
        we_bc = sb("we_bc", [P, H])
        eps_bc = sb("eps_bc", [P, 1])
        one_eps = sb("one_eps", [P, 1])
        gam = [sb(f"gam{i}", [P, CT]) for i in range(2)]
        bet = [sb(f"bet{i}", [P, CT]) for i in range(2)]
        b1 = sb("b1", [P, KT])
        ident = sb("ident", [P, P])
        ident_bf = sb("ident_bf", [P, P], BF16)
        diag_eps = sb("diag_eps", [P, P])
        nhalf = sb("nhalf", [P, 2, NT])
        neg_max = sb("neg_max", [P, UNITS])
        row_sum = sb("row_sum", [P, UNITS])
        row_inv = sb("row_inv", [P, UNITS])
        r_bc = sb("r_bc", [P, 2, P])
        bn6 = sb("bn6", [P, NT, 6])
        mv = sb("mv", [P, NT, 2])
        var_e = sb("var_e", [P, 2, NT])
        rstd = sb("rstd", [P, 2, NT])
        d_part = sb("d_part", [P, NT, NH])
        deg = sb("deg", [P, 2, NT])
        deg0 = sb("deg0", [P, 2, NT])
        deg1 = sb("deg1", [P, 2, NT])
        degp = sb("degp", [P, 2, NT])
        s_deg = sb("s_deg", [P, 2, NT])
        ns_out = sb("ns_out", [P, NT])
        x0 = sb("x0", [P, NT, D])
        adj_n = sb("adj_n", [P, NT, N])
        big = place[0]
        place[0] += 2 * 4 * NT * N
        qs = at("qs", big, [P, H, N], F32R)
        ks = at("ks", big + 32 * KB, [P, H, N], F32R)
        adjT_hi = at("adjT_hi", big, [P, NT, N], F32R)
        adjT_lo = at("adjT_lo", big + 32 * KB, [P, NT, N], F32R)
        m = place[0]
        place[0] += 68 * KB
        assert place[0] <= nc.sbuf_usable_end, place[0]
        q_hi = at("q_hi", m, [P, CT, N], F32R)
        q_lo = at("q_lo", m + 8 * KB, [P, CT, N], F32R)
        k_hi = at("k_hi", m + 16 * KB, [P, CT, N], F32R)
        k_lo = at("k_lo", m + 24 * KB, [P, CT, N], F32R)
        xT = at("xT", m + 32 * KB, [P, CT, N], F32)
        pT = at("pT", m, [P, PT_SLOTS, NT, P], F32)
        prob = at("prob", m + 24 * KB, [P, 2, N], F32)
        logit = at("logit", m + 32 * KB, [P, 2, N], F32)
        bias = at("bias", m + 40 * KB, [P, 2, N], F32)
        mask = at("mask", m + 48 * KB, [P, 2, N], BF16)
        v_sb = at("v_sb", m + 52 * KB, [P, NT, D], F32)
        copied = at("copied", m + 52 * KB, [P, N], F32)
        oT = at("oT", m + 60 * KB, [P, CT, N], F32)
        res = at("res", m, [P, NT, D], F32)
        cur = at("cur", m + 8 * KB, [P, NT, D], F32)
        xn = at("xn", m + 16 * KB, [P, NT, D], F32)
        x3b = at("x3b", m + 16 * KB, [P, NT, D], F32)
        nT = at("nT", m + 24 * KB, [P, CT, N], F32)
        hT = at("hT", m + 24 * KB, [P, CT, N], F32)
        y_out = at("y_out", m + 24 * KB, [P, NT, D], F32)
        z_hi = at("z_hi", m + 32 * KB, [P, NT, D], F32R)
        z_lo = at("z_lo", m + 40 * KB, [P, NT, D], F32R)
        pre = at("pre", m + 48 * KB, [P, NT, D], F32)
        soft = at("soft", m + 56 * KB, [P, NT, D], F32)
        x2d = at("x2d", m + 56 * KB, [P, NT, D], F32)
        uT = at("uT", m + 48 * KB, [P, KT, N], F32)

        psum = ctx.enter_context(nc.psum_tensor("psum", [P, 8, HALF], F32))
        bank = [psum[:, i, :] for i in range(8)]

        def score_bank(n, half):
            return bank[2 * (n % 2) + half]

        def score_pair(n):
            return psum[:, 2 * (n % 2):2 * (n % 2) + 2, :].rearrange("p a j -> p (a j)")

        def sem(name):
            return ctx.enter_context(nc.semaphore(name))

        def tally(name, per_batch, base=0):
            return Tally(sem(name), per_batch, base)

        WEIGHT_DMAS = 19
        CONSTS = 5
        weights_in = sem("weights_in")
        consts = sem("consts")
        pool_passed = sem("pool_passed")
        dve_passed = sem("dve_passed")
        ident_zero = sem("ident_zero")
        ident_done = sem("ident_done")
        x_in = tally("x_in", 16)
        adj_in = [tally(f"adj_in{i}", 16) for i in range(NP)]
        qk_stacked = tally("qk_stacked", 2 * 4 * G * 16)
        out_stored = tally("out_stored", 16, base=16)
        xT_ps = tally("xT_ps", 4)
        xT_act = tally("xT_act", 2)
        xT_dve = tally("xT_dve", 2)
        qk_ps = tally("qk_ps", 8)
        qk_hi = tally("qk_hi", 8)
        qk_lo = tally("qk_lo", 8)
        v_ps = tally("v_ps", 4)
        v_act = tally("v_act", 2)
        v_dve = tally("v_dve", 2)
        mask_done = tally("mask_done", NT)
        bias_done = tally("bias_done", UNITS)
        din_act = tally("din_act", NT // 2)
        din_dve = tally("din_dve", NT // 2)
        scores = tally("scores", UNITS)
        logits = tally("logits", UNITS)
        probs = tally("probs", UNITS)
        pT_ps = tally("pT_ps", 2 * UNITS)
        pT_act = tally("pT_act", UNITS)
        pT_dve = tally("pT_dve", UNITS)
        rinv_done = tally("rinv_done", GROUPS)
        av = tally("av", GROUPS)
        r_bc_done = tally("r_bc_done", GROUPS)
        o_norm = tally("o_norm", GROUPS)
        y0_ps = tally("y0_ps", NP)
        adjT_ps = tally("adjT_ps", NT * NH)
        adjT_hi_done = tally("adjT_hi_done", NT * NH)
        adjT_lo_done = tally("adjT_lo_done", NT * NH)
        dout_done = tally("dout_done", 1)
        deg_steps = tally("deg_steps", 5)
        summed = [tally(f"summed{i}", NP, base=NP if i == 3 else 0) for i in range(4)]
        bn_done = [tally(f"bn_done{i}", NT) for i in range(4)]
        mv_done = [tally(f"mv_done{i}", NT) for i in range(4)]
        var_done = [tally(f"var_done{i}", 2 if i < 2 else 1) for i in range(4)]
        rstd_done = [tally(f"rstd_done{i}", 1) for i in range(4)]
        xn_done = [tally(f"xn_done{i}", NT) for i in range(2)]
        cur_done = [tally(f"cur_done{i}", NT) for i in range(3)]
        nT_ps = [tally(f"nT_ps{i}", 4) for i in range(2)]
        nT_act = [tally(f"nT_act{i}", 2) for i in range(2)]
        nT_dve = [tally(f"nT_dve{i}", 2) for i in range(2)]
        zs_ps = tally("zs_ps", NT)
        self_sb = tally("self_sb", NT)
        z_hi_done = [tally("z_hi_done0", NT), tally("z_hi_done1", NP), tally("z_hi_done2", NP)]
        z_lo_done = [tally("z_lo_done0", NT), tally("z_lo_done1", NP), tally("z_lo_done2", NP)]
        agg_ps = tally("agg_ps", NP)
        pre_done = tally("pre_done", NT)
        abs_done = tally("abs_done", NP)
        exp_done = tally("exp_done", NP)
        ln_done = tally("ln_done", NP)
        relu_done = tally("relu_done", NP)
        z2_ps = tally("z2_ps", NP)
        conv_ps = tally("conv_ps", NP)
        conv_b = tally("conv_b", NP)
        x2d_done = tally("x2d_done", NP)
        x3b_done = tally("x3b_done", NT)
        h_ps = tally("h_ps", 4)
        h_act = tally("h_act", 2)
        h_dve = tally("h_dve", 2)
        u_ps = tally("u_ps", KT * NH)
        u_act = tally("u_act", KT * NH // 2)
        u_dve = tally("u_dve", KT * NH // 2)
        y3_ps = tally("y3_ps", NP)
        y_done = tally("y_done", NT)

        def rows(t, pair):
            return t[:, 2 * pair:2 * pair + 2, :]

        def bank_pair(i):
            return bank[i][:, :].rearrange("p (t d) -> p t d", t=2)

        def both(eng, v):
            return v[:, :].unsqueeze(1).to_broadcast([P, 2, D])

        block = ctx.enter_context(nc.Block())

        @block.sync
        def _(sp):
            def load_weights():
                n = 0
                for dst, src in ((wq, W_qT), (wk, W_kT), (wv, W_vT), (wo, W_oT), (w_rel, L2_W_rel),
                                 (w_root, L2_W_root), (w1, L3_W1), (w2, L3_W2)):
                    sp.dma_start(dst, src.rearrange("(t p) n -> p t n", p=P)).then_inc(weights_in, 16)
                    n += 1
                for i, src in enumerate((L1_W_neigh, L1_W_self)):
                    sp.dma_start(w_ns[:, :, i, :], src.rearrange("(t p) n -> p t n", p=P)).then_inc(weights_in, 16)
                    n += 1
                for dst, src in ((brel_bc, L2_b_rel), (b2_bc, L3_b2)):
                    sp.dma_start(dst, src.partition_broadcast(P)).then_inc(weights_in, 16)
                    n += 1
                sp.dma_start(we_bc, W_e.rearrange("h o -> (h o)").partition_broadcast(P)).then_inc(weights_in, 16)
                sp.dma_start(eps_bc, L3_eps.partition_broadcast(P)).then_inc(weights_in, 16)
                n += 2
                with nc.allow_non_contiguous_dma("per-partition vectors of a few hundred values"):
                    for dst, src in ((gam[0], L1_gamma), (bet[0], L1_beta), (gam[1], L2_gamma), (bet[1], L2_beta),
                                     (b1, L3_b1)):
                        sp.dma_start(dst, src.rearrange("(t p) -> p t", p=P)).then_inc(weights_in, 16)
                        n += 1
                assert n == WEIGHT_DMAS

            def load_batch(b):
                sp.dma_start(x0, x_t[b]).then_inc(x_in.sem, 16)
                for i in range(NP):
                    sp.dma_start(rows(adj_n, i), adj_t[b][:, 2 * i:2 * i + 2, :]).then_inc(adj_in[i].sem, 16)

            def stack_and_store(b, load_next):
                for first, dst, parts in ((0, qs, (q_hi, q_hi, q_lo, q_lo)), (4, ks, (k_hi, k_lo, k_hi, k_lo))):
                    sp.wait_ge(qk_hi.sem, qk_hi.at(b, first + 4))
                    sp.wait_ge(qk_lo.sem, qk_lo.at(b, first + 4))
                    for r in range(G):
                        for part, src in enumerate(parts):
                            sp.dma_start(dst[HD * part:HD * (part + 1), r::G, :].bitcast(F32),
                                         src[HD * r:HD * (r + 1), :, :].bitcast(F32)).then_inc(qk_stacked.sem, 16)
                if load_next:
                    sp.wait_ge(summed[0].sem, summed[0].at(b, NP))
                    sp.wait_ge(adjT_ps.sem, adjT_ps.at(b, NT * NH))
                    sp.wait_ge(din_act.sem, din_act.at(b, NT // 2))
                    sp.wait_ge(din_dve.sem, din_dve.at(b, NT // 2))
                    load_batch(b + 1)
                sp.wait_ge(y_done.sem, y_done.at(b, NT))
                sp.dma_start(out_t[b], y_out).then_inc(out_stored.sem, 16)

            load_weights()
            load_batch(0)
            with sp.Fori(0, B - 1) as b:
                stack_and_store(b, True)
            stack_and_store(B - 1, False)
            sp.wait_ge(out_stored.sem, out_stored.at(B - 1, 16))

        @block.gpsimd
        def _(pool):
            nc.gpsimd.memset(ident, 0.0).then_inc(ident_zero, 1)
            pool.wait_ge(ident_zero, 1)
            nc.gpsimd.affine_select(out=ident, in_=ident, compare_op=ALU.not_equal, fill=1.0, base=0,
                                    pattern=[[-1, P]], channel_multiplier=1).then_inc(ident_done, 1)
            pool.wait_ge(ident_done, 1)
            nc.gpsimd.tensor_copy(ident_bf, ident).then_inc(consts, 1)
            nc.gpsimd.memset(nhalf, -0.5).then_inc(consts, 1)
            pool.wait_ge(weights_in, 16 * WEIGHT_DMAS)
            nc.gpsimd.tensor_tensor(w_ns[:, :, 1, :], w_ns[:, :, 1, :], w_ns[:, :, 0, :], ALU.add).then_inc(consts, 1)
            nc.gpsimd.tensor_scalar(one_eps, eps_bc, 1.0, 1.0, ALU.mult, ALU.add).then_inc(consts, 1)
            pool.wait_ge(consts, 4)
            nc.gpsimd.tensor_scalar(diag_eps, ident, one_eps[:, 0:1], 0.0, ALU.mult, ALU.add).then_inc(consts, 1)

            def norm_root(b, l):
                kinds = 2 if l < 2 else 1
                pool.wait_ge(mv_done[l].sem, mv_done[l].at(b, NT))
                pool.sem_inc(pool_passed)
                nc.gpsimd.tensor_scalar(var_e[:, 0, :], mv[:, :, 1], 1.0, LN_EPS, ALU.mult, ALU.add)\
                    .then_inc(var_done[l].sem, 1)
                if kinds == 2:
                    nc.gpsimd.tensor_scalar(var_e[:, 1, :], mv[:, :, 1], 1.0 + LN_EPS, LN_EPS * LN_EPS, ALU.mult,
                                            ALU.add).then_inc(var_done[l].sem, 1)
                pool.wait_ge(var_done[l].sem, var_done[l].at(b, kinds))
                nc.gpsimd.tensor_tensor(rstd[:, 0:kinds, :], var_e[:, 0:kinds, :], nhalf[:, 0:kinds, :], ALU.pow)\
                    .then_inc(rstd_done[l].sem, 1)

            with pool.Fori(0, B) as b:
                for t in range(NT):
                    for h in range(H):
                        n = t * H + h
                        if n == 0:
                            pool.wait_ge(xT_ps.sem, xT_ps.at(b, 4))
                            pool.wait_ge(adj_in[0].sem, adj_in[0].at(b, 16))
                            pool.sem_inc(pool_passed)
                        if h == 0 and t % 2 == 0:
                            pool.wait_ge(adj_in[t // 2].sem, adj_in[t // 2].at(b, 16))
                            pool.sem_inc(pool_passed)
                        if n >= 2:
                            pool.wait_ge(logits.sem, logits.at(b, n - 1))
                            pool.sem_inc(pool_passed)
                        nc.gpsimd.tensor_scalar(bias[:, n % 2, :], adj_n[:, t, :], we_bc[:, h:h + 1], 0.0, ALU.mult,
                                                ALU.add).then_inc(bias_done.sem, 1)
                norm_root(b, 0)
                pool.wait_ge(dout_done.sem, dout_done.at(b, 1))
                pool.wait_ge(din_act.sem, din_act.at(b, NT // 2))
                pool.wait_ge(din_dve.sem, din_dve.at(b, NT // 2))
                pool.sem_inc(pool_passed)
                nc.gpsimd.tensor_scalar(deg0, deg, 0.0, 1.0, ALU.is_equal, ALU.mult).then_inc(deg_steps.sem, 1)
                pool.wait_ge(deg_steps.sem, deg_steps.at(b, 1))
                nc.gpsimd.tensor_tensor(deg1, deg, deg0, ALU.add).then_inc(deg_steps.sem, 1)
                pool.wait_ge(deg_steps.sem, deg_steps.at(b, 2))
                nc.gpsimd.tensor_tensor(degp, deg1, nhalf, ALU.pow).then_inc(deg_steps.sem, 1)
                pool.wait_ge(deg_steps.sem, deg_steps.at(b, 3))
                nc.gpsimd.tensor_tensor(s_deg, degp, deg0, ALU.subtract).then_inc(deg_steps.sem, 1)
                pool.wait_ge(deg_steps.sem, deg_steps.at(b, 4))
                pool.sem_inc(pool_passed)
                nc.gpsimd.tensor_scalar(ns_out, s_deg[:, 1, :], -1.0, 0.0, ALU.mult, ALU.add).then_inc(deg_steps.sem, 1)
                norm_root(b, 1)
                for i in range(NP):
                    pool.wait_ge(cur_done[1].sem, cur_done[1].at(b, 2 * i + 2))
                    pool.sem_inc(pool_passed)
                    nc.gpsimd.tensor_scalar(rows(x2d, i), rows(cur, i), 2.0, 0.0, ALU.mult, ALU.add)\
                        .then_inc(x2d_done.sem, 1)
                norm_root(b, 2)
                for t in range(NT):
                    pool.wait_ge(cur_done[2].sem, cur_done[2].at(b, t + 1))
                    nc.gpsimd.tensor_tensor(x3b[:, t, :], cur[:, t, :], b2_bc, ALU.add).then_inc(x3b_done.sem, 1)
                norm_root(b, 3)

        @block.scalar
        def _(act):
            act.wait_ge(weights_in, 16 * WEIGHT_DMAS)
            with act.Fori(0, B) as b:
                for k in (0, 2):
                    act.wait_ge(xT_ps.sem, xT_ps.at(b, k + 1))
                    nc.scalar.activation(xT[:, k // 2, (k % 2) * HALF:(k % 2 + 1) * HALF], bank[k][:, :], ACT.Copy)\
                        .then_inc(xT_act.sem, 1)
                act.wait_ge(out_stored.sem, out_stored.at(b, 0))
                for k in range(8):
                    act.wait_ge(qk_ps.sem, qk_ps.at(b, k + 1))
                    dst = (q_hi, k_hi)[k // 4][:, k % 4 // 2, (k % 2) * HALF:(k % 2 + 1) * HALF]
                    nc.scalar.activation(dst, bank[(4 + k) % 8][:, :], ACT.Copy, scale=SCALE if k < 4 else 1.0)\
                        .then_inc(qk_hi.sem, 1)
                for k in (0, 2):
                    act.wait_ge(v_ps.sem, v_ps.at(b, k + 1))
                    nc.scalar.activation(rows(v_sb, k), bank_pair(4 + k), ACT.Copy).then_inc(v_act.sem, 1)

                for n in range(UNITS + 8):
                    if 1 <= n <= UNITS:
                        u = n - 1
                        act.wait_ge(logits.sem, logits.at(b, u + 1))
                        if u >= 2:
                            act.wait_ge(pT_ps.sem, pT_ps.at(b, 2 * (u - 1)))
                        nc.scalar.activation(prob[:, u % 2, :], logit[:, u % 2, :], ACT.Exp, scale=-1.0,
                                             bias=neg_max[:, u:u + 1], accum_out=row_sum[:, u:u + 1])\
                            .then_inc(probs.sem, 1)
                    if 2 <= n < UNITS + 2:
                        u = n - 2
                        act.wait_ge(pT_ps.sem, pT_ps.at(b, 2 * u + 1))
                        if u >= PT_SLOTS:
                            act.wait_ge(av.sem, av.at(b, (u - PT_SLOTS) // G + 1))
                        nc.scalar.activation(pT[:, u % PT_SLOTS, 0:TPH, :],
                                             bank[4][:, :].rearrange("p (j i) -> p j i", j=TPH), ACT.Copy)\
                            .then_inc(pT_act.sem, 1)
                    if n >= 7 and (n - 7) % G == 0 and (n - 7) // G < GROUPS:
                        g = (n - 7) // G
                        act.wait_ge(av.sem, av.at(b, g + 1))
                        if g >= 2:
                            act.wait_ge(o_norm.sem, o_norm.at(b, g - 1))
                        nc.scalar.activation(r_bc[:, g % 2, :], bank[6 + g % 2][:, P:2 * P], ACT.Copy)\
                            .then_inc(r_bc_done.sem, 1)

                act.wait_ge(av.sem, av.at(b, GROUPS))
                for t in range(0, NT, 2):
                    if t:
                        act.wait_ge(din_act.sem, din_act.at(b, t // 2))
                    nc.scalar.activation(copied, adj_n[:, t, :], ACT.Copy, accum_out=deg[:, 0, t:t + 1])\
                        .then_inc(din_act.sem, 1)

                for k in range(NT * NH):
                    act.wait_ge(adjT_ps.sem, adjT_ps.at(b, k + 1))
                    half, j = k // NT, k % NT
                    nc.scalar.activation(adjT_hi[:, j, half * HALF:(half + 1) * HALF], bank[4 + k % 4][:, :],
                                         ACT.Identity, accum_out=d_part[:, j, half:half + 1])\
                        .then_inc(adjT_hi_done.sem, 1)

                def norm_transposed(l, first):
                    for k in (0, 2):
                        act.wait_ge(nT_ps[l].sem, nT_ps[l].at(b, k + 1))
                        c = k // 2
                        nc.scalar.activation(nT[:, c, (k % 2) * HALF:(k % 2 + 1) * HALF], bank[first + k][:, :],
                                             ACT.Identity, scale=gam[l][:, c:c + 1], bias=bet[l][:, c:c + 1])\
                            .then_inc(nT_act[l].sem, 1)

                norm_transposed(0, 0)
                for t in range(NT):
                    act.wait_ge(zs_ps.sem, zs_ps.at(b, t + 1))
                    nc.scalar.activation(pre[:, t, :], bank[4 + t % 4][:, D:2 * D], ACT.Copy).then_inc(self_sb.sem, 1)
                    if t == 0:
                        act.wait_ge(deg_steps.sem, deg_steps.at(b, 4))
                    nc.scalar.activation(z_hi[:, t, :], bank[4 + t % 4][:, 0:D], ACT.Copy, scale=s_deg[:, 0, t:t + 1])\
                        .then_inc(z_hi_done[0].sem, 1)
                for i in range(NP):
                    act.wait_ge(pre_done.sem, pre_done.at(b, 2 * i + 2))
                    nc.scalar.activation(rows(soft, i), rows(pre, i), ACT.Abs).then_inc(abs_done.sem, 1)
                    act.wait_ge(abs_done.sem, abs_done.at(b, i + 1))
                    nc.scalar.activation(rows(soft, i), rows(soft, i), ACT.Exp, scale=-1.0).then_inc(exp_done.sem, 1)
                    act.wait_ge(exp_done.sem, exp_done.at(b, i + 1))
                    nc.scalar.activation(rows(soft, i), rows(soft, i), ACT.Ln, bias=1.0).then_inc(ln_done.sem, 1)
                norm_transposed(1, 4)
                for i in range(NP):
                    act.wait_ge(z2_ps.sem, z2_ps.at(b, i + 1))
                    nc.scalar.activation(rows(z_hi, i), bank_pair(i), ACT.Copy).then_inc(z_hi_done[1].sem, 1)
                for i in range(NP):
                    act.wait_ge(cur_done[2].sem, cur_done[2].at(b, 2 * i + 2))
                    nc.scalar.activation(rows(z_hi, i), rows(cur, i), ACT.Copy).then_inc(z_hi_done[2].sem, 1)
                for k in (0, 2):
                    act.wait_ge(h_ps.sem, h_ps.at(b, k + 1))
                    nc.scalar.activation(hT[:, k % 2, (k // 2) * HALF:(k // 2 + 1) * HALF], bank[k][:, :], ACT.Copy)\
                        .then_inc(h_act.sem, 1)
                for k in range(0, KT * NH, 2):
                    act.wait_ge(u_ps.sem, u_ps.at(b, k + 1))
                    nc.scalar.activation(uT[:, k % KT, (k // KT) * HALF:(k // KT + 1) * HALF], bank[4 + k % 4][:, :],
                                         ACT.Relu, bias=b1[:, k % KT:k % KT + 1]).then_inc(u_act.sem, 1)

        @block.vector
        def _(dve):
            dve.wait_ge(weights_in, 16 * WEIGHT_DMAS)
            nc.vector.memset(row_sum, 0.0).then_inc(summed[3].sem, NP)
            nc.vector.memset(row_inv, 0.0).then_inc(out_stored.sem, 16)
            with dve.Fori(0, B) as b:
                for k in (1, 3):
                    dve.wait_ge(xT_ps.sem, xT_ps.at(b, k + 1))
                    nc.vector.tensor_copy(xT[:, k // 2, (k % 2) * HALF:(k % 2 + 1) * HALF], bank[k][:, :])\
                        .then_inc(xT_dve.sem, 1)
                dve.wait_ge(out_stored.sem, out_stored.at(b, 0))
                for k in range(8):
                    dve.wait_ge(qk_hi.sem, qk_hi.at(b, k + 1))
                    hi, lo = ((q_hi, q_lo), (k_hi, k_lo))[k // 4]
                    cols = slice((k % 2) * HALF, (k % 2 + 1) * HALF)
                    nc.vector.scalar_tensor_tensor(lo[:, k % 4 // 2, cols], bank[(4 + k) % 8][:, :],
                                                   SCALE if k < 4 else 1.0, hi[:, k % 4 // 2, cols].bitcast(F32),
                                                   ALU.mult, ALU.subtract).then_inc(qk_lo.sem, 1)
                for k in (1, 3):
                    dve.wait_ge(v_ps.sem, v_ps.at(b, k + 1))
                    nc.vector.tensor_copy(rows(v_sb, k), bank_pair(4 + k)).then_inc(v_dve.sem, 1)

                def make_mask(t):
                    if t % 2 == 0:
                        dve.wait_ge(adj_in[t // 2].sem, adj_in[t // 2].at(b, 16))
                    if t >= 2:
                        dve.wait_ge(scores.sem, scores.at(b, (t - 1) * H))
                    nc.vector.tensor_scalar(mask[:, t % 2, :], adj_n[:, t, :], 0.0, MASKED, ALU.is_equal, ALU.mult)\
                        .then_inc(mask_done.sem, 1)

                make_mask(0)
                for n in range(UNITS + 8):
                    if n < UNITS:
                        dve.wait_ge(bias_done.sem, bias_done.at(b, n + 1))
                        dve.wait_ge(scores.sem, scores.at(b, n + 1))
                        if n >= 2:
                            dve.wait_ge(probs.sem, probs.at(b, n - 1))
                        dve.sem_inc(dve_passed)
                        nc.vector.tensor_tensor_reduce(logit[:, n % 2, :], score_pair(n), bias[:, n % 2, :], -1.0, 3e38, ALU.add,
                                                       ALU.min, neg_max[:, n:n + 1]).then_inc(logits.sem, 1)
                    if n % H == 3 and n // H + 1 < NT:
                        make_mask(n // H + 1)
                    if 2 <= n < UNITS + 2:
                        u = n - 2
                        dve.wait_ge(pT_ps.sem, pT_ps.at(b, 2 * u + 2))
                        if u >= PT_SLOTS:
                            dve.wait_ge(av.sem, av.at(b, (u - PT_SLOTS) // G + 1))
                        nc.vector.tensor_copy(pT[:, u % PT_SLOTS, TPH:NT, :],
                                              bank[5][:, :].rearrange("p (j i) -> p j i", j=TPH))\
                            .then_inc(pT_dve.sem, 1)
                    if n >= 5 and (n - 5) % G == 0 and (n - 5) // G < GROUPS:
                        g = (n - 5) // G
                        dve.wait_ge(probs.sem, probs.at(b, G * g + G))
                        nc.vector.reciprocal(row_inv[:, G * g:G * g + G], row_sum[:, G * g:G * g + G])\
                            .then_inc(rinv_done.sem, 1)
                    if n >= 7 and (n - 7) % G == 0 and (n - 7) // G < GROUPS:
                        g = (n - 7) // G
                        dve.wait_ge(r_bc_done.sem, r_bc_done.at(b, g + 1))
                        t, hg = g // HG, g % HG
                        nc.vector.tensor_tensor(oT[:, hg, t * P:(t + 1) * P], bank[6 + g % 2][:, 0:P],
                                                r_bc[:, g % 2, :], ALU.mult).then_inc(o_norm.sem, 1)

                def row_stats(l, i):
                    dve.wait_ge(summed[l].sem, summed[l].at(b, i + 1))
                    for t in (2 * i, 2 * i + 1):
                        nc.vector.bn_stats(bn6[:, t, :], res[:, t, :]).then_inc(bn_done[l].sem, 1)

                def row_moments(l):
                    dve.wait_ge(bn_done[l].sem, bn_done[l].at(b, NT))
                    dve.sem_inc(dve_passed)
                    for t in range(NT):
                        nc.vector.bn_aggr(mv[:, t, :], bn6[:, t, :]).then_inc(mv_done[l].sem, 1)

                def normalise(l, kind, dst, done):
                    dve.wait_ge(rstd_done[l].sem, rstd_done[l].at(b, 1))
                    for t in range(NT):
                        nc.vector.tensor_scalar(dst[:, t, :], res[:, t, :], mv[:, t, 0:1], rstd[:, kind, t:t + 1],
                                                ALU.subtract, ALU.mult).then_inc(done.sem, 1)

                def adjT_low(k):
                    dve.wait_ge(adjT_hi_done.sem, adjT_hi_done.at(b, k + 1))
                    half, j = k // NT, k % NT
                    cols = slice(half * HALF, (half + 1) * HALF)
                    nc.vector.tensor_tensor(adjT_lo[:, j, cols], bank[4 + k % 4][:, :],
                                            adjT_hi[:, j, cols].bitcast(F32), ALU.subtract)\
                        .then_inc(adjT_lo_done.sem, 1)

                def norm_transposed(l, first):
                    for k in (1, 3):
                        dve.wait_ge(nT_ps[l].sem, nT_ps[l].at(b, k + 1))
                        c = k // 2
                        nc.vector.tensor_scalar(nT[:, c, (k % 2) * HALF:(k % 2 + 1) * HALF], bank[first + k][:, :],
                                                gam[l][:, c:c + 1], bet[l][:, c:c + 1], ALU.mult, ALU.add)\
                            .then_inc(nT_dve[l].sem, 1)

                for t in range(1, NT, 2):
                    nc.vector.tensor_reduce(deg[:, 0, t:t + 1], adj_n[:, t, :], AX.X, ALU.add).then_inc(din_dve.sem, 1)
                for i in range(NP):
                    dve.wait_ge(y0_ps.sem, y0_ps.at(b, i + 1))
                    nc.vector.tensor_tensor(rows(res, i), bank_pair(i), rows(x0, i), ALU.add).then_inc(summed[0].sem, 1)
                for i in range(NP):
                    row_stats(0, i)
                row_moments(0)
                for k in range(4):
                    adjT_low(k)
                normalise(0, 1, xn, xn_done[0])
                for k in range(4, NT * NH):
                    adjT_low(k)
                nc.vector.tensor_tensor(deg[:, 1, :], d_part[:, :, 0], d_part[:, :, 1], ALU.add)\
                    .then_inc(dout_done.sem, 1)
                norm_transposed(0, 0)
                normalise(0, 0, cur, cur_done[0])
                for t in range(NT):
                    dve.wait_ge(z_hi_done[0].sem, z_hi_done[0].at(b, t + 1))
                    nc.vector.scalar_tensor_tensor(z_lo[:, t, :], bank[4 + t % 4][:, 0:D], s_deg[:, 0, t:t + 1],
                                                   z_hi[:, t, :].bitcast(F32), ALU.mult, ALU.subtract)\
                        .then_inc(z_lo_done[0].sem, 1)
                dve.wait_ge(deg_steps.sem, deg_steps.at(b, 5))
                for i in range(NP):
                    dve.wait_ge(agg_ps.sem, agg_ps.at(b, i + 1))
                    for t in (2 * i, 2 * i + 1):
                        nc.vector.scalar_tensor_tensor(pre[:, t, :], bank[i][:, (t % 2) * D:(t % 2 + 1) * D],
                                                       ns_out[:, t:t + 1], pre[:, t, :], ALU.mult, ALU.add)\
                            .then_inc(pre_done.sem, 1)
                    if i == 0:
                        dve.wait_ge(cur_done[0].sem, cur_done[0].at(b, NT))
                    dve.wait_ge(abs_done.sem, abs_done.at(b, i + 1))
                    nc.vector.scalar_tensor_tensor(rows(pre, i), rows(pre, i), 0.0, rows(cur, i), ALU.max, ALU.add)\
                        .then_inc(relu_done.sem, 1)
                for i in range(NP):
                    dve.wait_ge(relu_done.sem, relu_done.at(b, i + 1))
                    dve.wait_ge(ln_done.sem, ln_done.at(b, i + 1))
                    nc.vector.tensor_tensor(rows(res, i), rows(pre, i), rows(soft, i), ALU.add)\
                        .then_inc(summed[1].sem, 1)
                    row_stats(1, i)
                row_moments(1)
                normalise(1, 1, xn, xn_done[1])
                normalise(1, 0, cur, cur_done[1])
                norm_transposed(1, 4)
                for i in range(NP):
                    dve.wait_ge(z_hi_done[1].sem, z_hi_done[1].at(b, i + 1))
                    nc.vector.tensor_tensor(rows(z_lo, i), bank_pair(i), rows(z_hi, i).bitcast(F32), ALU.subtract)\
                        .then_inc(z_lo_done[1].sem, 1)
                for i in range(NP):
                    dve.wait_ge(conv_ps.sem, conv_ps.at(b, i + 1))
                    nc.vector.tensor_tensor(rows(pre, i), bank_pair(4 + i), both(dve, brel_bc), ALU.add)\
                        .then_inc(conv_b.sem, 1)
                    dve.wait_ge(conv_b.sem, conv_b.at(b, i + 1))
                    dve.wait_ge(x2d_done.sem, x2d_done.at(b, i + 1))
                    nc.vector.scalar_tensor_tensor(rows(res, i), rows(pre, i), 0.0, rows(x2d, i), ALU.max, ALU.add)\
                        .then_inc(summed[2].sem, 1)
                    row_stats(2, i)
                row_moments(2)
                normalise(2, 0, cur, cur_done[2])
                for i in range(NP):
                    dve.wait_ge(z_hi_done[2].sem, z_hi_done[2].at(b, i + 1))
                    nc.vector.tensor_tensor(rows(z_lo, i), rows(cur, i), rows(z_hi, i).bitcast(F32), ALU.subtract)\
                        .then_inc(z_lo_done[2].sem, 1)
                for k in (1, 3):
                    dve.wait_ge(h_ps.sem, h_ps.at(b, k + 1))
                    nc.vector.tensor_copy(hT[:, k % 2, (k // 2) * HALF:(k // 2 + 1) * HALF], bank[k][:, :])\
                        .then_inc(h_dve.sem, 1)
                for k in range(1, KT * NH, 2):
                    dve.wait_ge(u_ps.sem, u_ps.at(b, k + 1))
                    nc.vector.tensor_scalar(uT[:, k % KT, (k // KT) * HALF:(k // KT + 1) * HALF], bank[4 + k % 4][:, :],
                                            b1[:, k % KT:k % KT + 1], 0.0, ALU.add, ALU.max).then_inc(u_dve.sem, 1)
                for i in range(NP):
                    dve.wait_ge(x3b_done.sem, x3b_done.at(b, 2 * i + 2))
                    dve.wait_ge(y3_ps.sem, y3_ps.at(b, i + 1))
                    nc.vector.tensor_tensor(rows(res, i), bank_pair(i), rows(x3b, i), ALU.add)\
                        .then_inc(summed[3].sem, 1)
                    row_stats(3, i)
                row_moments(3)
                normalise(3, 0, y_out, y_done)

        @block.tensor
        def _(pe):
            def split_product(dst, lhs_hi, lhs_lo, rhs_hi, rhs_lo, start, stop):
                nc.tensor.matmul(dst, lhs_hi, rhs_lo, start=start, stop=False)
                nc.tensor.matmul(dst, lhs_hi, rhs_hi, start=False, stop=False)
                return nc.tensor.matmul(dst, lhs_lo, rhs_hi, start=False, stop=stop)

            def rows_transposed(src, first, ready, done, b):
                for k in range(CT * NH):
                    c, half = k // NH, k % NH
                    for j in range(TPH):
                        t = half * TPH + j
                        if ready is not None and k < NH:
                            pe.wait_ge(ready.sem, ready.at(b, t + 1))
                        last = nc.tensor.transpose(bank[first + k][:, j * P:(j + 1) * P],
                                                   src[:, t, c * P:(c + 1) * P], ident)
                    last.then_inc(done.sem, 1)

            pe.wait_ge(consts, CONSTS)
            pe.wait_ge(weights_in, 16 * WEIGHT_DMAS)
            with pe.Fori(0, B) as b:
                pe.wait_ge(x_in.sem, x_in.at(b, 16))
                pe.wait_ge(summed[3].sem, summed[3].at(b, 0))
                rows_transposed(x0, 0, None, xT_ps, b)
                pe.wait_ge(xT_act.sem, xT_act.at(b, 2))
                pe.wait_ge(xT_dve.sem, xT_dve.at(b, 2))
                for k in range(8):
                    w, cg, half = (wq, wk)[k // 4], k % 4 // 2, k % 2
                    if k >= 4:
                        pass
                    for c in range(CT):
                        last = nc.tensor.matmul(bank[(4 + k) % 8][:, :], w[:, c, cg * P:(cg + 1) * P],
                                                xT[:, c, half * HALF:(half + 1) * HALF], start=c == 0, stop=c == CT - 1)
                    last.then_inc(qk_ps.sem, 1)
                for i in range(NP):
                    pe.wait_ge(qk_lo.sem, qk_lo.at(b, i + 1))
                    for t in (2 * i, 2 * i + 1):
                        for c in range(CT):
                            last = nc.tensor.matmul(bank[4 + i][:, (t % 2) * D:(t % 2 + 1) * D],
                                                    xT[:, c, t * P:(t + 1) * P], wv[:, c, :],
                                                    start=c == 0, stop=c == CT - 1)
                    last.then_inc(v_ps.sem, 1)

                pe.wait_ge(qk_stacked.sem, qk_stacked.at(b, 2 * 4 * G * 16))
                pe.wait_ge(v_act.sem, v_act.at(b, 2))
                pe.wait_ge(v_dve.sem, v_dve.at(b, 2))
                for n in range(UNITS + 6):
                    if n < UNITS:
                        t, h = n // H, n % H
                        if h == 0:
                            pe.wait_ge(mask_done.sem, mask_done.at(b, t + 1))
                        if n >= 2:
                            pe.wait_ge(logits.sem, logits.at(b, n - 1))
                        for half in range(NH):
                            cols = slice(half * HALF, (half + 1) * HALF)
                            nc.tensor.matmul(score_bank(n, half)[:, :], ident_bf, mask[:, t % 2, cols],
                                             start=True, stop=False)
                            last = nc.tensor.matmul(score_bank(n, half)[:, :], qs[:, h, t * P:(t + 1) * P],
                                                    ks[:, h, cols], start=False, stop=True)
                        last.then_inc(scores.sem, 1)
                    if 2 <= n < UNITS + 2:
                        u = n - 2
                        pe.wait_ge(probs.sem, probs.at(b, u + 1))
                        for half, freed in enumerate((pT_act, pT_dve)):
                            if u >= 1:
                                pe.wait_ge(freed.sem, freed.at(b, u))
                            for j in range(TPH):
                                jt = half * TPH + j
                                last = nc.tensor.transpose(bank[4 + half][:, j * P:(j + 1) * P],
                                                           prob[:, u % 2, jt * P:(jt + 1) * P], ident)
                            last.then_inc(pT_ps.sem, 1)
                    if n >= 6 and (n - 6) % G == 0 and (n - 6) // G < GROUPS:
                        g = (n - 6) // G
                        pe.wait_ge(pT_act.sem, pT_act.at(b, G * g + G))
                        pe.wait_ge(pT_dve.sem, pT_dve.at(b, G * g + G))
                        pe.wait_ge(rinv_done.sem, rinv_done.at(b, g + 1))
                        if g >= 2:
                            pe.wait_ge(o_norm.sem, o_norm.at(b, g - 1))
                        for j in range(NT):
                            for r in range(G):
                                u = G * g + r
                                h = u % H
                                nc.tensor.matmul(bank[6 + g % 2][HD * r:HD * (r + 1), 0:P],
                                                 v_sb[:, j, h * HD:(h + 1) * HD], pT[:, u % PT_SLOTS, j, :],
                                                 start=j == 0, stop=j == NT - 1)
                        for r in range(G):
                            u = G * g + r
                            last = nc.tensor.matmul(bank[6 + g % 2][HD * r:HD * (r + 1), P:2 * P],
                                                    row_inv[:, u:u + 1].to_broadcast([P, HD]), ident,
                                                    start=True, stop=True)
                        last.then_inc(av.sem, 1)

                pe.wait_ge(logits.sem, logits.at(b, UNITS))
                for i in range(NP):
                    pe.wait_ge(o_norm.sem, o_norm.at(b, HG * (2 * i + 2)))
                    for t in (2 * i, 2 * i + 1):
                        for c in range(CT):
                            last = nc.tensor.matmul(bank[i][:, (t % 2) * D:(t % 2 + 1) * D],
                                                    oT[:, c, t * P:(t + 1) * P], wo[:, c, :],
                                                    start=c == 0, stop=c == CT - 1)
                    last.then_inc(y0_ps.sem, 1)
                pe.wait_ge(pT_act.sem, pT_act.at(b, UNITS))
                pe.wait_ge(pT_dve.sem, pT_dve.at(b, UNITS))
                for k in range(NT * NH):
                    half, j = k // NT, k % NT
                    if k >= 4:
                        pe.wait_ge(adjT_lo_done.sem, adjT_lo_done.at(b, k - 3))
                    for i in range(TPH):
                        last = nc.tensor.transpose(bank[4 + k % 4][:, i * P:(i + 1) * P],
                                                   adj_n[:, half * TPH + i, j * P:(j + 1) * P], ident)
                    last.then_inc(adjT_ps.sem, 1)

                def aggregate(dst, t, start):
                    for j in range(NT):
                        rws = slice(t * P, (t + 1) * P)
                        last = split_product(dst, adjT_hi[:, j, rws], adjT_lo[:, j, rws], z_hi[:, j, :], z_lo[:, j, :],
                                             start and j == 0, j == NT - 1)
                    return last

                rows_transposed(xn, 0, xn_done[0], nT_ps[0], b)
                pe.wait_ge(nT_act[0].sem, nT_act[0].at(b, 2))
                pe.wait_ge(nT_dve[0].sem, nT_dve[0].at(b, 2))
                for t in range(NT):
                    if t < 4:
                        pe.wait_ge(adjT_lo_done.sem, adjT_lo_done.at(b, NT * NH - 3 + t))
                    else:
                        pe.wait_ge(z_lo_done[0].sem, z_lo_done[0].at(b, t - 3))
                    for c in range(CT):
                        last = nc.tensor.matmul(bank[4 + t % 4][:, :], nT[:, c, t * P:(t + 1) * P],
                                                w_ns[:, c, :, :].rearrange("p a d -> p (a d)"),
                                                start=c == 0, stop=c == CT - 1)
                    last.then_inc(zs_ps.sem, 1)
                pe.wait_ge(z_lo_done[0].sem, z_lo_done[0].at(b, NT))
                for i in range(NP):
                    for t in (2 * i, 2 * i + 1):
                        last = aggregate(bank[i][:, (t % 2) * D:(t % 2 + 1) * D], t, True)
                    last.then_inc(agg_ps.sem, 1)
                rows_transposed(xn, 4, xn_done[1], nT_ps[1], b)
                pe.wait_ge(nT_act[1].sem, nT_act[1].at(b, 2))
                pe.wait_ge(nT_dve[1].sem, nT_dve[1].at(b, 2))
                for i in range(NP):
                    for t in (2 * i, 2 * i + 1):
                        for c in range(CT):
                            last = nc.tensor.matmul(bank[i][:, (t % 2) * D:(t % 2 + 1) * D],
                                                    nT[:, c, t * P:(t + 1) * P], w_rel[:, c, :],
                                                    start=c == 0, stop=c == CT - 1)
                    last.then_inc(z2_ps.sem, 1)
                pe.wait_ge(z_lo_done[1].sem, z_lo_done[1].at(b, NP))
                for i in range(NP):
                    for t in (2 * i, 2 * i + 1):
                        dst = bank[4 + i][:, (t % 2) * D:(t % 2 + 1) * D]
                        for c in range(CT):
                            nc.tensor.matmul(dst, nT[:, c, t * P:(t + 1) * P], w_root[:, c, :], start=c == 0, stop=False)
                        last = aggregate(dst, t, False)
                    last.then_inc(conv_ps.sem, 1)
                pe.wait_ge(cur_done[2].sem, cur_done[2].at(b, NT))
                pe.wait_ge(z_lo_done[2].sem, z_lo_done[2].at(b, NP))
                for k in range(CT * NH):
                    half, c = k // CT, k % CT
                    feats = slice(c * P, (c + 1) * P)
                    cols = slice(half * HALF, (half + 1) * HALF)
                    for j in range(NT):
                        split_product(bank[k][:, :], z_hi[:, j, feats], z_lo[:, j, feats], adjT_hi[:, j, cols],
                                      adjT_lo[:, j, cols], j == 0, False)
                    for i in range(TPH):
                        last = nc.tensor.matmul(bank[k][:, i * P:(i + 1) * P], cur[:, half * TPH + i, feats], diag_eps,
                                                start=False, stop=i == TPH - 1)
                    last.then_inc(h_ps.sem, 1)
                for k in range(KT * NH):
                    half, o = k // KT, k % KT
                    if o == 0:
                        pe.wait_ge(h_act.sem, h_act.at(b, half + 1))
                        pe.wait_ge(h_dve.sem, h_dve.at(b, half + 1))
                    if k >= 4:
                        pe.wait_ge((u_act, u_dve)[k % 2].sem, (u_act, u_dve)[k % 2].at(b, (k - 4) // 2 + 1))
                    for c in range(CT):
                        last = nc.tensor.matmul(bank[4 + k % 4][:, :], w1[:, c, o * P:(o + 1) * P],
                                                hT[:, c, half * HALF:(half + 1) * HALF], start=c == 0, stop=c == CT - 1)
                    last.then_inc(u_ps.sem, 1)
                for i in range(NP):
                    if i % (NP // NH) == 0:
                        half = i // (NP // NH)
                        pe.wait_ge(u_act.sem, u_act.at(b, (half + 1) * KT // 2))
                        pe.wait_ge(u_dve.sem, u_dve.at(b, (half + 1) * KT // 2))
                    for t in (2 * i, 2 * i + 1):
                        for c in range(KT):
                            last = nc.tensor.matmul(bank[i][:, (t % 2) * D:(t % 2 + 1) * D],
                                                    uT[:, c, t * P:(t + 1) * P], w2[:, c, :],
                                                    start=c == 0, stop=c == KT - 1)
                    last.then_inc(y3_ps.sem, 1)


_INS = ["x", "adj", "L0_gnn_W_q", "L0_gnn_W_k", "L0_gnn_W_v", "L0_gnn_W_e", "L0_gnn_W_o", "L1_gnn_gamma",
        "L1_gnn_beta", "L1_gnn_W_self", "L1_gnn_W_neigh", "L2_gnn_W_rel", "L2_gnn_b_rel", "L2_gnn_W_root",
        "L2_gnn_ln_gamma", "L2_gnn_ln_beta", "L3_gnn_eps", "L3_gnn_W1", "L3_gnn_b1", "L3_gnn_W2", "L3_gnn_b2"]
_TRANSPOSED = ("L0_gnn_W_q", "L0_gnn_W_k", "L0_gnn_W_v", "L0_gnn_W_o")


def kernel(**inputs):
    import numpy as _np
    import concourse.bacc as _bacc
    from concourse import mybir as _mybir
    from concourse.bass_utils import run_bass_kernel_spmd as _run

    nc = _bacc.Bacc("TRN2", target_bir_lowering=False, num_devices=1)
    arrays, args = {}, []
    for name in _INS:
        a = _np.asarray(inputs[name])
        a = _np.ascontiguousarray(a.T if name in _TRANSPOSED else a)
        arrays[f"in_{name}_dram"] = a
        args.append(nc.dram_tensor(f"in_{name}_dram", a.shape, _mybir.dt.from_np(a.dtype), kind="ExternalInput").ap())
    shape = tuple(inputs["x"].shape)
    args.append(nc.dram_tensor("out_0_dram", shape, _mybir.dt.from_np(_np.dtype("float32")), kind="ExternalOutput").ap())
    gnn_stack_kernel(nc, *args)
    r = _run(nc, [arrays], core_ids=[0])
    return r.results[0]["out_0_dram"]
```

```python
from contextlib import ExitStack

import concourse.bass as bass
from concourse import mybir

F32 = mybir.dt.float32
F32R = mybir.dt.float32r
BF16 = mybir.dt.bfloat16
ALU = mybir.AluOpType
ACT = mybir.ActivationFunctionType
AX = mybir.AxisListType

P = 128
LN_EPS = 1e-5
MASKED = -1e30
KB = 1024


class Tally:

    def __init__(self, sem, per_batch, base=0):
        self.sem, self.per_batch, self.base = sem, per_batch, base

    def at(self, b, count):
        return b * self.per_batch + (self.base + count)


def gnn_stack_kernel(nc: bass.Bass, x, adj, W_qT, W_kT, W_vT, W_e, W_oT, L1_gamma, L1_beta, L1_W_self, L1_W_neigh,
                     L2_W_rel, L2_b_rel, L2_W_root, L2_gamma, L2_beta, L3_eps, L3_W1, L3_b1, L3_W2, L3_b2, out):
    B, N, D = x.shape
    H = W_e.shape[0]
    HD = D // H
    HID = L3_W1.shape[1]
    NT = N // P
    CT = D // P
    KT = HID // P
    HALF = 512
    NH = N // HALF
    TPH = HALF // P
    NP = NT // 2
    G = P // HD
    HG = H // G
    UNITS = NT * H
    GROUPS = UNITS // G
    PT_SLOTS = 6
    SCALE = float(HD) ** -0.5
    assert 2 * D == HALF and G * HD == P and 4 * HD == P

    x_t = x.rearrange("b (t p) d -> b p t d", p=P)
    out_t = out.rearrange("b (t p) d -> b p t d", p=P)
    adj_t = adj.rearrange("b (t p) j -> b p t j", p=P)

    ctx = ExitStack()
    with ctx:
        place = [(nc.sbuf_base + 63) // 64 * 64]

        def at(name, offset, shape, dt):
            return nc.alloc_sbuf_tensor_at(name, shape, dt, offset=offset).ap()

        def sb(name, shape, dt=F32):
            size = 2 if dt == BF16 else 4
            for n in shape[1:]:
                size *= n
            offset = place[0]
            place[0] += (size + 63) // 64 * 64
            return at(name, offset, shape, dt)

        wq = sb("wq", [P, CT, D])
        wk = sb("wk", [P, CT, D])
        wv = sb("wv", [P, CT, D])
        wo = sb("wo", [P, CT, D])
        w_ns = sb("w_ns", [P, CT, 2, D])
        w_rel = sb("w_rel", [P, CT, D])
        w_root = sb("w_root", [P, CT, D])
        w1 = sb("w1", [P, CT, HID])
        w2 = sb("w2", [P, KT, D])
        brel_bc = sb("brel_bc", [P, D])
        b2_bc = sb("b2_bc", [P, D])
        we_bc = sb("we_bc", [P, H])
        eps_bc = sb("eps_bc", [P, 1])
        one_eps = sb("one_eps", [P, 1])
        gam = [sb(f"gam{i}", [P, CT]) for i in range(2)]
        bet = [sb(f"bet{i}", [P, CT]) for i in range(2)]
        b1 = sb("b1", [P, KT])
        ident = sb("ident", [P, P])
        ident_bf = sb("ident_bf", [P, P], BF16)
        diag_eps = sb("diag_eps", [P, P])
        nhalf = sb("nhalf", [P, 2, NT])
        neg_max = sb("neg_max", [P, UNITS])
        row_sum = sb("row_sum", [P, UNITS])
        row_inv = sb("row_inv", [P, UNITS])
        r_bc = sb("r_bc", [P, 2, P])
        bn6 = sb("bn6", [P, NT, 6])
        mv = sb("mv", [P, NT, 2])
        var_e = sb("var_e", [P, 2, NT])
        rstd = sb("rstd", [P, 2, NT])
        d_part = sb("d_part", [P, NT, NH])
        deg = sb("deg", [P, 2, NT])
        deg0 = sb("deg0", [P, 2, NT])
        deg1 = sb("deg1", [P, 2, NT])
        degp = sb("degp", [P, 2, NT])
        s_deg = sb("s_deg", [P, 2, NT])
        ns_out = sb("ns_out", [P, NT])
        x0 = sb("x0", [P, NT, D])
        rows_at = place[0]
        adj_n = sb("adj_n", [P, NT, N])
        q_hi = at("q_hi", rows_at, [P, CT, N], F32R)
        q_lo = at("q_lo", rows_at + 8 * KB, [P, CT, N], F32R)
        k_hi = at("k_hi", rows_at + 16 * KB, [P, CT, N], F32R)
        k_lo = at("k_lo", rows_at + 24 * KB, [P, CT, N], F32R)
        big = place[0]
        place[0] += 2 * 4 * NT * N
        qs = at("qs", big, [P, H, N], F32R)
        ks = at("ks", big + 32 * KB, [P, H, N], F32R)
        adjT_hi = at("adjT_hi", big, [P, NT, N], F32R)
        adjT_lo = at("adjT_lo", big + 32 * KB, [P, NT, N], F32R)
        m = place[0]
        place[0] += 68 * KB
        assert place[0] <= nc.sbuf_usable_end, place[0]
        pT = at("pT", m, [P, PT_SLOTS, NT, P], F32)
        prob = at("prob", m + 24 * KB, [P, 2, N], F32)
        logit = at("logit", m + 32 * KB, [P, 2, N], F32)
        bias = at("bias", m + 40 * KB, [P, 2, N], F32)
        mask = at("mask", m + 48 * KB, [P, 2, N], BF16)
        v_sb = at("v_sb", m + 52 * KB, [P, NT, D], F32)
        oT = at("oT", m + 60 * KB, [P, CT, N], F32)
        res = at("res", m, [P, NT, D], F32)
        cur = at("cur", m + 8 * KB, [P, NT, D], F32)
        xn = at("xn", m + 16 * KB, [P, NT, D], F32)
        xT = at("xT", m + 16 * KB, [P, CT, N], F32)
        nT = at("nT", m + 24 * KB, [P, CT, N], F32)
        hT = at("hT", m + 24 * KB, [P, CT, N], F32)
        y_out = at("y_out", m + 24 * KB, [P, NT, D], F32)
        z_hi = at("z_hi", m + 32 * KB, [P, NT, D], F32R)
        z_lo = at("z_lo", m + 40 * KB, [P, NT, D], F32R)
        pre = at("pre", m + 48 * KB, [P, NT, D], F32)
        soft = at("soft", m + 56 * KB, [P, NT, D], F32)
        x2d = at("x2d", m + 56 * KB, [P, NT, D], F32)
        uT = at("uT", m + 48 * KB, [P, KT, N], F32)

        psum = ctx.enter_context(nc.psum_tensor("psum", [P, 8, HALF], F32))
        bank = [psum[:, i, :] for i in range(8)]

        def score_bank(n, half):
            return bank[2 * (n % 2) + half]

        def score_pair(n):
            return psum[:, 2 * (n % 2):2 * (n % 2) + 2, :].rearrange("p a j -> p (a j)")

        def sem(name):
            return ctx.enter_context(nc.semaphore(name))

        def tally(name, per_batch, base=0):
            return Tally(sem(name), per_batch, base)

        WEIGHT_DMAS = 19
        CONSTS = 5
        weights_in = sem("weights_in")
        consts = sem("consts")
        pool_passed = sem("pool_passed")
        dve_passed = sem("dve_passed")
        ident_zero = sem("ident_zero")
        ident_done = sem("ident_done")
        x_in = tally("x_in", 16)
        adj_in = [tally(f"adj_in{i}", 16) for i in range(NP)]
        q_stacked = tally("q_stacked", 4 * G * 16)
        k_stacked = tally("k_stacked", 4 * G * 16)
        out_stored = tally("out_stored", 32, base=32)
        xT_ps = tally("xT_ps", 4)
        xT_act = tally("xT_act", 2)
        xT_dve = tally("xT_dve", 2)
        qk_ps = tally("qk_ps", 8)
        qk_hi = tally("qk_hi", 8)
        qk_lo = tally("qk_lo", 8)
        v_ps = tally("v_ps", 4)
        v_act = tally("v_act", 2)
        v_dve = tally("v_dve", 2)
        mask_done = tally("mask_done", NT)
        bias_done = tally("bias_done", UNITS)
        din_done = tally("din_done", NT)
        scores = tally("scores", UNITS)
        logits = tally("logits", UNITS)
        probs = tally("probs", UNITS)
        pT_ps = tally("pT_ps", 2 * UNITS)
        pT_act = tally("pT_act", UNITS)
        pT_dve = tally("pT_dve", UNITS)
        rinv_done = tally("rinv_done", GROUPS)
        av = tally("av", GROUPS)
        r_bc_done = tally("r_bc_done", GROUPS)
        o_norm = tally("o_norm", GROUPS)
        y0_ps = tally("y0_ps", NP)
        adjT_ps = tally("adjT_ps", NT * NH)
        adjT_hi_done = tally("adjT_hi_done", NT * NH)
        adjT_lo_done = tally("adjT_lo_done", NT * NH)
        dout_done = tally("dout_done", 1)
        deg_steps = tally("deg_steps", 5)
        summed = [tally(f"summed{i}", NP, base=NP if i == 3 else 0) for i in range(4)]
        bn_done = [tally(f"bn_done{i}", NT) for i in range(4)]
        mv_done = [tally(f"mv_done{i}", NT) for i in range(4)]
        var_done = [tally(f"var_done{i}", 4 if i < 2 else 2) for i in range(4)]
        rstd_done = [tally(f"rstd_done{i}", 2) for i in range(4)]
        xn_done = [tally(f"xn_done{i}", NT) for i in range(2)]
        cur_done = [tally(f"cur_done{i}", NT) for i in range(3)]
        nT_ps = [tally(f"nT_ps{i}", 4) for i in range(2)]
        nT_act = [tally(f"nT_act{i}", 2) for i in range(2)]
        nT_dve = [tally(f"nT_dve{i}", 2) for i in range(2)]
        zs_ps = tally("zs_ps", NT)
        self_sb = tally("self_sb", NT)
        z_hi_done = [tally("z_hi_done0", NT), tally("z_hi_done1", NP), tally("z_hi_done2", NP)]
        z_lo_done = [tally("z_lo_done0", NT), tally("z_lo_done1", NP), tally("z_lo_done2", NP)]
        agg_ps = tally("agg_ps", NP)
        pre_done = tally("pre_done", NT)
        abs_done = tally("abs_done", NP)
        exp_done = tally("exp_done", NP)
        ln_done = tally("ln_done", NP)
        relu_done = tally("relu_done", NP)
        z2_ps = tally("z2_ps", NP)
        conv_ps = tally("conv_ps", NP)
        conv_b = tally("conv_b", NP)
        x2d_done = tally("x2d_done", NP)
        b2_added = tally("b2_added", NT)
        h_ps = tally("h_ps", 4)
        h_act = tally("h_act", 2)
        h_dve = tally("h_dve", 2)
        u_ps = tally("u_ps", KT * NH)
        u_act = tally("u_act", KT * NH // 2)
        u_dve = tally("u_dve", KT * NH // 2)
        y3_ps = tally("y3_ps", NP)
        y_done = tally("y_done", NT)

        def rows(t, pair):
            return t[:, 2 * pair:2 * pair + 2, :]

        def bank_pair(i):
            return bank[i][:, :].rearrange("p (t d) -> p t d", t=2)

        def over_pair(v):
            return v[:, :].unsqueeze(1).to_broadcast([P, 2, D])

        block = ctx.enter_context(nc.Block())

        @block.sync
        def _(sp):
            def load_weights():
                n = 0
                for dst, src in ((wq, W_qT), (wk, W_kT), (wv, W_vT), (wo, W_oT), (w_rel, L2_W_rel),
                                 (w_root, L2_W_root), (w1, L3_W1), (w2, L3_W2)):
                    sp.dma_start(dst, src.rearrange("(t p) n -> p t n", p=P)).then_inc(weights_in, 16)
                    n += 1
                for i, src in enumerate((L1_W_neigh, L1_W_self)):
                    sp.dma_start(w_ns[:, :, i, :], src.rearrange("(t p) n -> p t n", p=P)).then_inc(weights_in, 16)
                    n += 1
                for dst, src in ((brel_bc, L2_b_rel), (b2_bc, L3_b2)):
                    sp.dma_start(dst, src.partition_broadcast(P)).then_inc(weights_in, 16)
                    n += 1
                sp.dma_start(we_bc, W_e.rearrange("h o -> (h o)").partition_broadcast(P)).then_inc(weights_in, 16)
                sp.dma_start(eps_bc, L3_eps.partition_broadcast(P)).then_inc(weights_in, 16)
                n += 2
                with nc.allow_non_contiguous_dma("per-partition vectors of a few hundred values"):
                    for dst, src in ((gam[0], L1_gamma), (bet[0], L1_beta), (gam[1], L2_gamma), (bet[1], L2_beta),
                                     (b1, L3_b1)):
                        sp.dma_start(dst, src.rearrange("(t p) -> p t", p=P)).then_inc(weights_in, 16)
                        n += 1
                assert n == WEIGHT_DMAS

            def load_x(b):
                sp.dma_start(x0, x_t[b]).then_inc(x_in.sem, 16)

            def stack(b, first, dst, parts, stacked):
                sp.wait_ge(qk_hi.sem, qk_hi.at(b, first + 4))
                sp.wait_ge(qk_lo.sem, qk_lo.at(b, first + 4))
                for r in range(G):
                    for part, src in enumerate(parts):
                        sp.dma_start(dst[HD * part:HD * (part + 1), r::G, :].bitcast(F32),
                                     src[HD * r:HD * (r + 1), :, :].bitcast(F32)).then_inc(stacked.sem, 16)

            def enter_batch(b):
                stack(b, 0, qs, (q_hi, q_hi, q_lo, q_lo), q_stacked)
                stack(b, 4, ks, (k_hi, k_lo, k_hi, k_lo), k_stacked)
                for i in range(NP):
                    if i == 0:
                        sp.wait_ge(q_stacked.sem, q_stacked.at(b, 4 * G * 16))
                    if i == NP // 2:
                        sp.wait_ge(k_stacked.sem, k_stacked.at(b, 4 * G * 16))
                    sp.dma_start(rows(adj_n, i), adj_t[b][:, 2 * i:2 * i + 2, :]).then_inc(adj_in[i].sem, 16)

            def leave_batch(b, has_next):
                if has_next:
                    sp.wait_ge(summed[0].sem, summed[0].at(b, NP))
                    load_x(b + 1)
                    sp.wait_ge(h_ps.sem, h_ps.at(b, 4))
                    enter_batch(b + 1)
                for half in range(NH):
                    sp.wait_ge(y_done.sem, y_done.at(b, TPH * (half + 1)))
                    ts = slice(half * TPH, (half + 1) * TPH)
                    sp.dma_start(out_t[b][:, ts, :], y_out[:, ts, :]).then_inc(out_stored.sem, 16)

            load_weights()
            load_x(0)
            enter_batch(0)
            with sp.Fori(0, B - 1) as b:
                leave_batch(b, True)
            leave_batch(B - 1, False)
            sp.wait_ge(out_stored.sem, out_stored.at(B - 1, 32))

        @block.gpsimd
        def _(pool):
            nc.gpsimd.memset(ident, 0.0).then_inc(ident_zero, 1)
            pool.wait_ge(ident_zero, 1)
            nc.gpsimd.affine_select(out=ident, in_=ident, compare_op=ALU.not_equal, fill=1.0, base=0,
                                    pattern=[[-1, P]], channel_multiplier=1).then_inc(ident_done, 1)
            pool.wait_ge(ident_done, 1)
            nc.gpsimd.tensor_copy(ident_bf, ident).then_inc(consts, 1)
            nc.gpsimd.memset(nhalf, -0.5).then_inc(consts, 1)
            pool.wait_ge(weights_in, 16 * WEIGHT_DMAS)
            nc.gpsimd.tensor_tensor(w_ns[:, :, 1, :], w_ns[:, :, 1, :], w_ns[:, :, 0, :], ALU.add).then_inc(consts, 1)
            nc.gpsimd.tensor_scalar(one_eps, eps_bc, 1.0, 1.0, ALU.mult, ALU.add).then_inc(consts, 1)
            pool.wait_ge(consts, 4)
            nc.gpsimd.tensor_scalar(diag_eps, ident, one_eps[:, 0:1], 0.0, ALU.mult, ALU.add).then_inc(consts, 1)

            def norm_root(b, l, half):
                kinds = 2 if l < 2 else 1
                ts = slice(half * TPH, (half + 1) * TPH)
                pool.wait_ge(mv_done[l].sem, mv_done[l].at(b, TPH * (half + 1)))
                pool.sem_inc(pool_passed)
                nc.gpsimd.tensor_scalar(var_e[:, 0, ts], mv[:, ts, 1], 1.0, LN_EPS, ALU.mult, ALU.add)\
                    .then_inc(var_done[l].sem, 1)
                if kinds == 2:
                    nc.gpsimd.tensor_scalar(var_e[:, 1, ts], mv[:, ts, 1], 1.0 + LN_EPS, LN_EPS * LN_EPS, ALU.mult,
                                            ALU.add).then_inc(var_done[l].sem, 1)
                pool.wait_ge(var_done[l].sem, var_done[l].at(b, kinds * (half + 1)))
                nc.gpsimd.tensor_tensor(rstd[:, 0:kinds, ts], var_e[:, 0:kinds, ts], nhalf[:, 0:kinds, ts], ALU.pow)\
                    .then_inc(rstd_done[l].sem, 1)

            with pool.Fori(0, B) as b:
                for n in range(UNITS):
                    t, h = n // H, n % H
                    if h == 0 and t % 2 == 0:
                        pool.wait_ge(adj_in[t // 2].sem, adj_in[t // 2].at(b, 16))
                        pool.sem_inc(pool_passed)
                    if n >= 2:
                        pool.wait_ge(logits.sem, logits.at(b, n - 1))
                        pool.sem_inc(pool_passed)
                    nc.gpsimd.tensor_scalar(bias[:, n % 2, :], adj_n[:, t, :], we_bc[:, h:h + 1], 0.0, ALU.mult,
                                            ALU.add).then_inc(bias_done.sem, 1)
                for half in range(NH):
                    norm_root(b, 0, half)
                pool.wait_ge(din_done.sem, din_done.at(b, NT))
                pool.wait_ge(dout_done.sem, dout_done.at(b, 1))
                pool.sem_inc(pool_passed)
                nc.gpsimd.tensor_scalar(deg0, deg, 0.0, 1.0, ALU.is_equal, ALU.mult).then_inc(deg_steps.sem, 1)
                pool.wait_ge(deg_steps.sem, deg_steps.at(b, 1))
                nc.gpsimd.tensor_tensor(deg1, deg, deg0, ALU.add).then_inc(deg_steps.sem, 1)
                pool.wait_ge(deg_steps.sem, deg_steps.at(b, 2))
                nc.gpsimd.tensor_tensor(degp, deg1, nhalf, ALU.pow).then_inc(deg_steps.sem, 1)
                pool.wait_ge(deg_steps.sem, deg_steps.at(b, 3))
                nc.gpsimd.tensor_tensor(s_deg, degp, deg0, ALU.subtract).then_inc(deg_steps.sem, 1)
                pool.wait_ge(deg_steps.sem, deg_steps.at(b, 4))
                pool.sem_inc(pool_passed)
                nc.gpsimd.tensor_scalar(ns_out, s_deg[:, 1, :], -1.0, 0.0, ALU.mult, ALU.add).then_inc(deg_steps.sem, 1)
                for half in range(NH):
                    norm_root(b, 1, half)
                    for i in range(half * NP // NH, (half + 1) * NP // NH):
                        pool.wait_ge(cur_done[1].sem, cur_done[1].at(b, 2 * i + 2))
                        pool.sem_inc(pool_passed)
                        nc.gpsimd.tensor_scalar(rows(x2d, i), rows(cur, i), 2.0, 0.0, ALU.mult, ALU.add)\
                            .then_inc(x2d_done.sem, 1)
                for half in range(NH):
                    norm_root(b, 2, half)
                pool.wait_ge(h_ps.sem, h_ps.at(b, 4))
                for t in range(NT):
                    nc.gpsimd.tensor_tensor(cur[:, t, :], cur[:, t, :], b2_bc, ALU.add).then_inc(b2_added.sem, 1)
                for half in range(NH):
                    norm_root(b, 3, half)

        @block.scalar
        def _(act):
            act.wait_ge(weights_in, 16 * WEIGHT_DMAS)
            nc.scalar.preload_act_table_set("natural_log_exp_and_others")

            def transpose_x(b):
                for k in (0, 2):
                    act.wait_ge(xT_ps.sem, xT_ps.at(b, k + 1))
                    nc.scalar.activation(xT[:, k % CT, (k // CT) * HALF:(k // CT + 1) * HALF], bank[k], ACT.Copy)\
                        .then_inc(xT_act.sem, 1)

            def project(b, first, hi, scale):
                for k in range(4):
                    act.wait_ge(qk_ps.sem, qk_ps.at(b, first + k + 1))
                    nc.scalar.activation(hi[:, k // 2, (k % 2) * HALF:(k % 2 + 1) * HALF], bank[first + k], ACT.Copy,
                                         scale=scale).then_inc(qk_hi.sem, 1)

            def project_v(b):
                for k in (0, 2):
                    act.wait_ge(v_ps.sem, v_ps.at(b, k + 1))
                    nc.scalar.activation(rows(v_sb, k), bank_pair(4 + k), ACT.Copy).then_inc(v_act.sem, 1)

            def batch(b, has_next):
                for n in range(UNITS + 8):
                    if 1 <= n <= UNITS:
                        u = n - 1
                        act.wait_ge(logits.sem, logits.at(b, u + 1))
                        if u == 0:
                            act.wait_ge(out_stored.sem, out_stored.at(b, 0))
                        if u >= 2:
                            act.wait_ge(pT_ps.sem, pT_ps.at(b, 2 * (u - 1)))
                        nc.scalar.activation(prob[:, u % 2, :], logit[:, u % 2, :], ACT.Exp, scale=-1.0,
                                             bias=neg_max[:, u:u + 1], accum_out=row_sum[:, u:u + 1])\
                            .then_inc(probs.sem, 1)
                    if 2 <= n < UNITS + 2:
                        u = n - 2
                        act.wait_ge(pT_ps.sem, pT_ps.at(b, 2 * u + 1))
                        if u >= PT_SLOTS:
                            act.wait_ge(av.sem, av.at(b, (u - PT_SLOTS) // G + 1))
                        nc.scalar.activation(pT[:, u % PT_SLOTS, 0:TPH, :],
                                             bank[4][:, :].rearrange("p (j i) -> p j i", j=TPH), ACT.Copy)\
                            .then_inc(pT_act.sem, 1)
                    if n >= 7 and (n - 7) % G == 0 and (n - 7) // G < GROUPS:
                        g = (n - 7) // G
                        act.wait_ge(av.sem, av.at(b, g + 1))
                        if g >= 2:
                            act.wait_ge(o_norm.sem, o_norm.at(b, g - 1))
                        nc.scalar.activation(r_bc[:, g % 2, :], bank[6 + g % 2][:, P:2 * P], ACT.Copy)\
                            .then_inc(r_bc_done.sem, 1)

                for k in range(NT * NH):
                    act.wait_ge(adjT_ps.sem, adjT_ps.at(b, k + 1))
                    half, j = k // NT, k % NT
                    nc.scalar.activation(adjT_hi[:, j, half * HALF:(half + 1) * HALF], bank[4 + k % 4][:, :],
                                         ACT.Identity, accum_out=d_part[:, j, half:half + 1])\
                        .then_inc(adjT_hi_done.sem, 1)

                def norm_transposed(l, first):
                    for k in (0, 2):
                        act.wait_ge(nT_ps[l].sem, nT_ps[l].at(b, k + 1))
                        c = k % CT
                        nc.scalar.activation(nT[:, c, (k // CT) * HALF:(k // CT + 1) * HALF], bank[first + k][:, :],
                                             ACT.Identity, scale=gam[l][:, c:c + 1], bias=bet[l][:, c:c + 1])\
                            .then_inc(nT_act[l].sem, 1)

                norm_transposed(0, 0)
                for t in range(NT):
                    act.wait_ge(zs_ps.sem, zs_ps.at(b, t + 1))
                    nc.scalar.activation(pre[:, t, :], bank[4 + t % 4][:, D:2 * D], ACT.Copy).then_inc(self_sb.sem, 1)
                    if t == 0:
                        act.wait_ge(deg_steps.sem, deg_steps.at(b, 4))
                    nc.scalar.activation(z_hi[:, t, :], bank[4 + t % 4][:, 0:D], ACT.Copy, scale=s_deg[:, 0, t:t + 1])\
                        .then_inc(z_hi_done[0].sem, 1)
                for i in range(NP):
                    act.wait_ge(pre_done.sem, pre_done.at(b, 2 * i + 2))
                    nc.scalar.activation(rows(soft, i), rows(pre, i), ACT.Abs).then_inc(abs_done.sem, 1)
                    act.wait_ge(abs_done.sem, abs_done.at(b, i + 1))
                    nc.scalar.activation(rows(soft, i), rows(soft, i), ACT.Exp, scale=-1.0).then_inc(exp_done.sem, 1)
                    act.wait_ge(exp_done.sem, exp_done.at(b, i + 1))
                    nc.scalar.activation(rows(soft, i), rows(soft, i), ACT.Ln, bias=1.0).then_inc(ln_done.sem, 1)
                norm_transposed(1, 4)
                for i in range(NP):
                    act.wait_ge(z2_ps.sem, z2_ps.at(b, i + 1))
                    nc.scalar.activation(rows(z_hi, i), bank_pair(i), ACT.Copy).then_inc(z_hi_done[1].sem, 1)
                if has_next:
                    transpose_x(b + 1)
                    project(b + 1, 0, q_hi, SCALE)
                act.wait_ge(conv_ps.sem, conv_ps.at(b, NP))
                for i in range(NP):
                    act.wait_ge(cur_done[2].sem, cur_done[2].at(b, 2 * i + 2))
                    nc.scalar.activation(rows(z_hi, i), rows(cur, i), ACT.Copy).then_inc(z_hi_done[2].sem, 1)
                if has_next:
                    project(b + 1, 4, k_hi, 1.0)
                for k in (0, 2):
                    act.wait_ge(h_ps.sem, h_ps.at(b, k + 1))
                    nc.scalar.activation(hT[:, k % 2, (k // 2) * HALF:(k // 2 + 1) * HALF], bank[k][:, :], ACT.Copy)\
                        .then_inc(h_act.sem, 1)
                for k in range(0, KT * NH, 2):
                    act.wait_ge(u_ps.sem, u_ps.at(b, k + 1))
                    nc.scalar.activation(uT[:, k % KT, (k // KT) * HALF:(k // KT + 1) * HALF], bank[4 + k % 4][:, :],
                                         ACT.Relu, bias=b1[:, k % KT:k % KT + 1]).then_inc(u_act.sem, 1)
                if has_next:
                    project_v(b + 1)

            transpose_x(0)
            project(0, 0, q_hi, SCALE)
            project(0, 4, k_hi, 1.0)
            project_v(0)
            with act.Fori(0, B - 1) as b:
                batch(b, True)
            batch(B - 1, False)

        @block.vector
        def _(dve):
            dve.wait_ge(weights_in, 16 * WEIGHT_DMAS)
            nc.vector.memset(row_sum, 0.0).then_inc(summed[3].sem, NP)
            nc.vector.memset(row_inv, 0.0).then_inc(out_stored.sem, 32)

            def transpose_x(b):
                for k in (1, 3):
                    dve.wait_ge(xT_ps.sem, xT_ps.at(b, k + 1))
                    nc.vector.tensor_copy(xT[:, k % CT, (k // CT) * HALF:(k // CT + 1) * HALF], bank[k])\
                        .then_inc(xT_dve.sem, 1)

            def project(b, first, hi, lo, scale):
                for k in range(4):
                    dve.wait_ge(qk_hi.sem, qk_hi.at(b, first + k + 1))
                    cols = slice((k % 2) * HALF, (k % 2 + 1) * HALF)
                    nc.vector.scalar_tensor_tensor(lo[:, k // 2, cols], bank[first + k], scale,
                                                   hi[:, k // 2, cols].bitcast(F32), ALU.mult, ALU.subtract)\
                        .then_inc(qk_lo.sem, 1)

            def project_v(b):
                for k in (1, 3):
                    dve.wait_ge(v_ps.sem, v_ps.at(b, k + 1))
                    nc.vector.tensor_copy(rows(v_sb, k), bank_pair(4 + k)).then_inc(v_dve.sem, 1)

            def batch(b, has_next):
                def make_mask(t):
                    if t % 2 == 0:
                        dve.wait_ge(adj_in[t // 2].sem, adj_in[t // 2].at(b, 16))
                    if t >= 2:
                        dve.wait_ge(scores.sem, scores.at(b, (t - 1) * H))
                    nc.vector.tensor_scalar(mask[:, t % 2, :], adj_n[:, t, :], 0.0, MASKED, ALU.is_equal, ALU.mult)\
                        .then_inc(mask_done.sem, 1)
                    nc.vector.tensor_reduce(deg[:, 0, t:t + 1], adj_n[:, t, :], AX.X, ALU.add).then_inc(din_done.sem, 1)

                make_mask(0)
                for n in range(UNITS + 8):
                    if n < UNITS:
                        dve.wait_ge(bias_done.sem, bias_done.at(b, n + 1))
                        dve.wait_ge(scores.sem, scores.at(b, n + 1))
                        if n >= 2:
                            dve.wait_ge(probs.sem, probs.at(b, n - 1))
                        dve.sem_inc(dve_passed)
                        nc.vector.tensor_tensor_reduce(logit[:, n % 2, :], score_pair(n), bias[:, n % 2, :], -1.0, 3e38, ALU.add,
                                                       ALU.min, neg_max[:, n:n + 1]).then_inc(logits.sem, 1)
                    if n % H == 3 and n // H + 1 < NT:
                        make_mask(n // H + 1)
                    if 2 <= n < UNITS + 2:
                        u = n - 2
                        dve.wait_ge(pT_ps.sem, pT_ps.at(b, 2 * u + 2))
                        if u >= PT_SLOTS:
                            dve.wait_ge(av.sem, av.at(b, (u - PT_SLOTS) // G + 1))
                        nc.vector.tensor_copy(pT[:, u % PT_SLOTS, TPH:NT, :],
                                              bank[5][:, :].rearrange("p (j i) -> p j i", j=TPH))\
                            .then_inc(pT_dve.sem, 1)
                    if n >= 5 and (n - 5) % G == 0 and (n - 5) // G < GROUPS:
                        g = (n - 5) // G
                        dve.wait_ge(probs.sem, probs.at(b, G * g + G))
                        nc.vector.reciprocal(row_inv[:, G * g:G * g + G], row_sum[:, G * g:G * g + G])\
                            .then_inc(rinv_done.sem, 1)
                    if n >= 7 and (n - 7) % G == 0 and (n - 7) // G < GROUPS:
                        g = (n - 7) // G
                        dve.wait_ge(r_bc_done.sem, r_bc_done.at(b, g + 1))
                        t, hg = g // HG, g % HG
                        nc.vector.tensor_tensor(oT[:, hg, t * P:(t + 1) * P], bank[6 + g % 2][:, 0:P],
                                                r_bc[:, g % 2, :], ALU.mult).then_inc(o_norm.sem, 1)

                def row_stats(l, i):
                    dve.wait_ge(summed[l].sem, summed[l].at(b, i + 1))
                    for t in (2 * i, 2 * i + 1):
                        nc.vector.bn_stats(bn6[:, t, :], res[:, t, :]).then_inc(bn_done[l].sem, 1)

                def row_moments(l, half):
                    dve.wait_ge(bn_done[l].sem, bn_done[l].at(b, TPH * (half + 1)))
                    dve.sem_inc(dve_passed)
                    for t in range(half * TPH, (half + 1) * TPH):
                        nc.vector.bn_aggr(mv[:, t, :], bn6[:, t, :]).then_inc(mv_done[l].sem, 1)

                def normalise(l, half, kind, dst, done):
                    dve.wait_ge(rstd_done[l].sem, rstd_done[l].at(b, half + 1))
                    for t in range(half * TPH, (half + 1) * TPH):
                        nc.vector.tensor_scalar(dst[:, t, :], res[:, t, :], mv[:, t, 0:1], rstd[:, kind, t:t + 1],
                                                ALU.subtract, ALU.mult).then_inc(done.sem, 1)

                def adjT_low(k):
                    dve.wait_ge(adjT_hi_done.sem, adjT_hi_done.at(b, k + 1))
                    half, j = k // NT, k % NT
                    cols = slice(half * HALF, (half + 1) * HALF)
                    nc.vector.tensor_tensor(adjT_lo[:, j, cols], bank[4 + k % 4][:, :],
                                            adjT_hi[:, j, cols].bitcast(F32), ALU.subtract)\
                        .then_inc(adjT_lo_done.sem, 1)

                def norm_transposed(l, first):
                    for k in (1, 3):
                        dve.wait_ge(nT_ps[l].sem, nT_ps[l].at(b, k + 1))
                        c = k % CT
                        nc.vector.tensor_scalar(nT[:, c, (k // CT) * HALF:(k // CT + 1) * HALF], bank[first + k],
                                                gam[l][:, c:c + 1], bet[l][:, c:c + 1], ALU.mult, ALU.add)\
                            .then_inc(nT_dve[l].sem, 1)

                for i in range(NP):
                    dve.wait_ge(y0_ps.sem, y0_ps.at(b, i + 1))
                    nc.vector.tensor_tensor(rows(res, i), bank_pair(i), rows(x0, i), ALU.add).then_inc(summed[0].sem, 1)
                    row_stats(0, i)
                    if i % 2:
                        row_moments(0, i // 2)
                for k in range(4):
                    adjT_low(k)
                for half in range(NH):
                    normalise(0, half, 1, xn, xn_done[0])
                for k in range(4, NT * NH):
                    adjT_low(k)
                nc.vector.tensor_tensor(deg[:, 1, :], d_part[:, :, 0], d_part[:, :, 1], ALU.add)\
                    .then_inc(dout_done.sem, 1)
                norm_transposed(0, 0)
                for half in range(NH):
                    normalise(0, half, 0, cur, cur_done[0])
                for t in range(NT):
                    dve.wait_ge(z_hi_done[0].sem, z_hi_done[0].at(b, t + 1))
                    nc.vector.scalar_tensor_tensor(z_lo[:, t, :], bank[4 + t % 4][:, 0:D], s_deg[:, 0, t:t + 1],
                                                   z_hi[:, t, :].bitcast(F32), ALU.mult, ALU.subtract)\
                        .then_inc(z_lo_done[0].sem, 1)
                dve.wait_ge(deg_steps.sem, deg_steps.at(b, 5))
                dve.wait_ge(cur_done[0].sem, cur_done[0].at(b, NT))
                for i in range(NP):
                    dve.wait_ge(agg_ps.sem, agg_ps.at(b, i + 1))
                    for t in (2 * i, 2 * i + 1):
                        nc.vector.scalar_tensor_tensor(pre[:, t, :], bank[i][:, (t % 2) * D:(t % 2 + 1) * D],
                                                       ns_out[:, t:t + 1], pre[:, t, :], ALU.mult, ALU.add)\
                            .then_inc(pre_done.sem, 1)
                    dve.wait_ge(pre_done.sem, pre_done.at(b, 2 * i + 2))
                    dve.wait_ge(abs_done.sem, abs_done.at(b, i + 1))
                    nc.vector.scalar_tensor_tensor(rows(pre, i), rows(pre, i), 0.0, rows(cur, i), ALU.max, ALU.add)\
                        .then_inc(relu_done.sem, 1)
                    dve.wait_ge(relu_done.sem, relu_done.at(b, i + 1))
                    dve.wait_ge(ln_done.sem, ln_done.at(b, i + 1))
                    nc.vector.tensor_tensor(rows(res, i), rows(pre, i), rows(soft, i), ALU.add)\
                        .then_inc(summed[1].sem, 1)
                    row_stats(1, i)
                    if i % 2:
                        row_moments(1, i // 2)
                        normalise(1, i // 2, 1, xn, xn_done[1])
                        normalise(1, i // 2, 0, cur, cur_done[1])
                norm_transposed(1, 4)
                for i in range(NP):
                    dve.wait_ge(z_hi_done[1].sem, z_hi_done[1].at(b, i + 1))
                    nc.vector.tensor_tensor(rows(z_lo, i), bank_pair(i), rows(z_hi, i).bitcast(F32), ALU.subtract)\
                        .then_inc(z_lo_done[1].sem, 1)
                if has_next:
                    transpose_x(b + 1)
                for i in range(NP):
                    dve.wait_ge(conv_ps.sem, conv_ps.at(b, i + 1))
                    nc.vector.tensor_tensor(rows(pre, i), bank_pair(4 + i), over_pair(brel_bc), ALU.add)\
                        .then_inc(conv_b.sem, 1)
                    dve.wait_ge(conv_b.sem, conv_b.at(b, i + 1))
                    dve.wait_ge(x2d_done.sem, x2d_done.at(b, i + 1))
                    nc.vector.scalar_tensor_tensor(rows(res, i), rows(pre, i), 0.0, rows(x2d, i), ALU.max, ALU.add)\
                        .then_inc(summed[2].sem, 1)
                    row_stats(2, i)
                    if i % 2:
                        row_moments(2, i // 2)
                        normalise(2, i // 2, 0, cur, cur_done[2])
                if has_next:
                    project(b + 1, 0, q_hi, q_lo, SCALE)
                for i in range(NP):
                    dve.wait_ge(z_hi_done[2].sem, z_hi_done[2].at(b, i + 1))
                    nc.vector.tensor_tensor(rows(z_lo, i), rows(cur, i), rows(z_hi, i).bitcast(F32), ALU.subtract)\
                        .then_inc(z_lo_done[2].sem, 1)
                if has_next:
                    project(b + 1, 4, k_hi, k_lo, 1.0)
                for k in (1, 3):
                    dve.wait_ge(h_ps.sem, h_ps.at(b, k + 1))
                    nc.vector.tensor_copy(hT[:, k % 2, (k // 2) * HALF:(k // 2 + 1) * HALF], bank[k])\
                        .then_inc(h_dve.sem, 1)
                for k in range(1, KT * NH, 2):
                    dve.wait_ge(u_ps.sem, u_ps.at(b, k + 1))
                    nc.vector.tensor_scalar(uT[:, k % KT, (k // KT) * HALF:(k // KT + 1) * HALF], bank[4 + k % 4],
                                            b1[:, k % KT:k % KT + 1], 0.0, ALU.add, ALU.max).then_inc(u_dve.sem, 1)
                for i in range(NP):
                    dve.wait_ge(b2_added.sem, b2_added.at(b, 2 * i + 2))
                    dve.wait_ge(y3_ps.sem, y3_ps.at(b, i + 1))
                    nc.vector.tensor_tensor(rows(res, i), bank_pair(i), rows(cur, i), ALU.add)\
                        .then_inc(summed[3].sem, 1)
                    row_stats(3, i)
                    if i % 2:
                        row_moments(3, i // 2)
                        normalise(3, i // 2, 0, y_out, y_done)
                if has_next:
                    project_v(b + 1)

            transpose_x(0)
            project(0, 0, q_hi, q_lo, SCALE)
            project(0, 4, k_hi, k_lo, 1.0)
            project_v(0)
            with dve.Fori(0, B - 1) as b:
                batch(b, True)
            batch(B - 1, False)

        @block.tensor
        def _(pe):
            def split_product(dst, lhs_hi, lhs_lo, rhs_hi, rhs_lo, start, stop):
                nc.tensor.matmul(dst, lhs_hi, rhs_lo, start=start, stop=False)
                nc.tensor.matmul(dst, lhs_hi, rhs_hi, start=False, stop=False)
                return nc.tensor.matmul(dst, lhs_lo, rhs_hi, start=False, stop=stop)

            def rows_transposed(src, half, first, done):
                for c in range(CT):
                    for j in range(TPH):
                        last = nc.tensor.transpose(bank[first + half * CT + c][:, j * P:(j + 1) * P],
                                                   src[:, half * TPH + j, c * P:(c + 1) * P], ident)
                    last.then_inc(done.sem, 1)

            def transpose_x(b):
                pe.wait_ge(x_in.sem, x_in.at(b, 16))
                for half in range(NH):
                    rows_transposed(x0, half, 0, xT_ps)

            def project(b, k, w):
                for c in range(CT):
                    last = nc.tensor.matmul(bank[k], w[:, c, k % 4 // 2 * P:(k % 4 // 2 + 1) * P],
                                            xT[:, c, k % 2 * HALF:(k % 2 + 1) * HALF], start=c == 0, stop=c == CT - 1)
                last.then_inc(qk_ps.sem, 1)

            def project_v(b):
                for i in range(NP):
                    for t in (2 * i, 2 * i + 1):
                        for c in range(CT):
                            last = nc.tensor.matmul(bank[4 + i][:, (t % 2) * D:(t % 2 + 1) * D],
                                                    xT[:, c, t * P:(t + 1) * P], wv[:, c, :],
                                                    start=c == 0, stop=c == CT - 1)
                    last.then_inc(v_ps.sem, 1)

            def batch(b, has_next):
                pe.wait_ge(q_stacked.sem, q_stacked.at(b, 4 * G * 16))
                pe.wait_ge(k_stacked.sem, k_stacked.at(b, 4 * G * 16))
                pe.wait_ge(v_act.sem, v_act.at(b, 2))
                pe.wait_ge(v_dve.sem, v_dve.at(b, 2))
                pe.wait_ge(summed[3].sem, summed[3].at(b, 0))
                for n in range(UNITS + 6):
                    if n < UNITS:
                        t, h = n // H, n % H
                        if h == 0:
                            pe.wait_ge(mask_done.sem, mask_done.at(b, t + 1))
                        if n >= 2:
                            pe.wait_ge(logits.sem, logits.at(b, n - 1))
                        for half in range(NH):
                            cols = slice(half * HALF, (half + 1) * HALF)
                            nc.tensor.matmul(score_bank(n, half)[:, :], ident_bf, mask[:, t % 2, cols],
                                             start=True, stop=False)
                            last = nc.tensor.matmul(score_bank(n, half)[:, :], qs[:, h, t * P:(t + 1) * P],
                                                    ks[:, h, cols], start=False, stop=True)
                        last.then_inc(scores.sem, 1)
                    if 2 <= n < UNITS + 2:
                        u = n - 2
                        pe.wait_ge(probs.sem, probs.at(b, u + 1))
                        for half, freed in enumerate((pT_act, pT_dve)):
                            if u >= 1:
                                pe.wait_ge(freed.sem, freed.at(b, u))
                            for j in range(TPH):
                                jt = half * TPH + j
                                last = nc.tensor.transpose(bank[4 + half][:, j * P:(j + 1) * P],
                                                           prob[:, u % 2, jt * P:(jt + 1) * P], ident)
                            last.then_inc(pT_ps.sem, 1)
                    if n >= 6 and (n - 6) % G == 0 and (n - 6) // G < GROUPS:
                        g = (n - 6) // G
                        pe.wait_ge(pT_act.sem, pT_act.at(b, G * g + G))
                        pe.wait_ge(pT_dve.sem, pT_dve.at(b, G * g + G))
                        pe.wait_ge(rinv_done.sem, rinv_done.at(b, g + 1))
                        if g >= 2:
                            pe.wait_ge(o_norm.sem, o_norm.at(b, g - 1))
                        for j in range(NT):
                            for r in range(G):
                                u = G * g + r
                                h = u % H
                                nc.tensor.matmul(bank[6 + g % 2][HD * r:HD * (r + 1), 0:P],
                                                 v_sb[:, j, h * HD:(h + 1) * HD], pT[:, u % PT_SLOTS, j, :],
                                                 start=j == 0, stop=j == NT - 1)
                        for r in range(G):
                            u = G * g + r
                            last = nc.tensor.matmul(bank[6 + g % 2][HD * r:HD * (r + 1), P:2 * P],
                                                    row_inv[:, u:u + 1].to_broadcast([P, HD]), ident,
                                                    start=True, stop=True)
                        last.then_inc(av.sem, 1)

                pe.wait_ge(logits.sem, logits.at(b, UNITS))
                for i in range(NP):
                    pe.wait_ge(o_norm.sem, o_norm.at(b, HG * (2 * i + 2)))
                    for t in (2 * i, 2 * i + 1):
                        for c in range(CT):
                            last = nc.tensor.matmul(bank[i][:, (t % 2) * D:(t % 2 + 1) * D],
                                                    oT[:, c, t * P:(t + 1) * P], wo[:, c, :],
                                                    start=c == 0, stop=c == CT - 1)
                    last.then_inc(y0_ps.sem, 1)
                pe.wait_ge(pT_act.sem, pT_act.at(b, UNITS))
                pe.wait_ge(pT_dve.sem, pT_dve.at(b, UNITS))
                for k in range(NT * NH):
                    half, j = k // NT, k % NT
                    if k >= 4:
                        pe.wait_ge(adjT_lo_done.sem, adjT_lo_done.at(b, k - 3))
                    for i in range(TPH):
                        last = nc.tensor.transpose(bank[4 + k % 4][:, i * P:(i + 1) * P],
                                                   adj_n[:, half * TPH + i, j * P:(j + 1) * P], ident)
                    last.then_inc(adjT_ps.sem, 1)

                def aggregate(dst, t, start):
                    for j in range(NT):
                        rws = slice(t * P, (t + 1) * P)
                        last = split_product(dst, adjT_hi[:, j, rws], adjT_lo[:, j, rws], z_hi[:, j, :], z_lo[:, j, :],
                                             start and j == 0, j == NT - 1)
                    return last

                for half in range(NH):
                    pe.wait_ge(xn_done[0].sem, xn_done[0].at(b, TPH * (half + 1)))
                    rows_transposed(xn, half, 0, nT_ps[0])
                for t in range(NT):
                    if t % TPH == 0:
                        pe.wait_ge(nT_act[0].sem, nT_act[0].at(b, t // TPH + 1))
                        pe.wait_ge(nT_dve[0].sem, nT_dve[0].at(b, t // TPH + 1))
                    if t < 4:
                        pe.wait_ge(adjT_lo_done.sem, adjT_lo_done.at(b, NT * NH - 3 + t))
                    else:
                        pe.wait_ge(z_lo_done[0].sem, z_lo_done[0].at(b, t - 3))
                    for c in range(CT):
                        last = nc.tensor.matmul(bank[4 + t % 4][:, :], nT[:, c, t * P:(t + 1) * P],
                                                w_ns[:, c, :, :].rearrange("p a d -> p (a d)"),
                                                start=c == 0, stop=c == CT - 1)
                    last.then_inc(zs_ps.sem, 1)
                pe.wait_ge(z_lo_done[0].sem, z_lo_done[0].at(b, NT))
                for i in range(NP):
                    for t in (2 * i, 2 * i + 1):
                        last = aggregate(bank[i][:, (t % 2) * D:(t % 2 + 1) * D], t, True)
                    last.then_inc(agg_ps.sem, 1)
                for half in range(NH):
                    pe.wait_ge(xn_done[1].sem, xn_done[1].at(b, TPH * (half + 1)))
                    rows_transposed(xn, half, 4, nT_ps[1])
                    pe.wait_ge(nT_act[1].sem, nT_act[1].at(b, half + 1))
                    pe.wait_ge(nT_dve[1].sem, nT_dve[1].at(b, half + 1))
                    for i in range(half * NP // NH, (half + 1) * NP // NH):
                        for t in (2 * i, 2 * i + 1):
                            for c in range(CT):
                                last = nc.tensor.matmul(bank[i][:, (t % 2) * D:(t % 2 + 1) * D],
                                                        nT[:, c, t * P:(t + 1) * P], w_rel[:, c, :],
                                                        start=c == 0, stop=c == CT - 1)
                        last.then_inc(z2_ps.sem, 1)
                pe.wait_ge(z_lo_done[1].sem, z_lo_done[1].at(b, NP))
                if has_next:
                    transpose_x(b + 1)
                for i in range(NP):
                    for t in (2 * i, 2 * i + 1):
                        dst = bank[4 + i][:, (t % 2) * D:(t % 2 + 1) * D]
                        for c in range(CT):
                            nc.tensor.matmul(dst, nT[:, c, t * P:(t + 1) * P], w_root[:, c, :], start=c == 0, stop=False)
                        last = aggregate(dst, t, False)
                    last.then_inc(conv_ps.sem, 1)
                if has_next:
                    pe.wait_ge(xT_act.sem, xT_act.at(b + 1, 2))
                    pe.wait_ge(xT_dve.sem, xT_dve.at(b + 1, 2))
                    for k in range(4):
                        project(b + 1, k, wq)
                    for k in range(4, 8):
                        pe.wait_ge(conv_b.sem, conv_b.at(b, k - 3))
                        project(b + 1, k, wk)
                    pe.wait_ge(qk_lo.sem, qk_lo.at(b + 1, 4))
                pe.wait_ge(cur_done[2].sem, cur_done[2].at(b, NT))
                pe.wait_ge(z_lo_done[2].sem, z_lo_done[2].at(b, NP))
                for k in range(CT * NH):
                    half, c = k // CT, k % CT
                    feats = slice(c * P, (c + 1) * P)
                    cols = slice(half * HALF, (half + 1) * HALF)
                    for j in range(NT):
                        split_product(bank[k][:, :], z_hi[:, j, feats], z_lo[:, j, feats], adjT_hi[:, j, cols],
                                      adjT_lo[:, j, cols], j == 0, False)
                    for i in range(TPH):
                        last = nc.tensor.matmul(bank[k][:, i * P:(i + 1) * P], cur[:, half * TPH + i, feats], diag_eps,
                                                start=False, stop=i == TPH - 1)
                    last.then_inc(h_ps.sem, 1)
                if has_next:
                    pe.wait_ge(qk_lo.sem, qk_lo.at(b + 1, 8))
                for k in range(KT * NH):
                    half, o = k // KT, k % KT
                    if o == 0:
                        pe.wait_ge(h_act.sem, h_act.at(b, half + 1))
                        pe.wait_ge(h_dve.sem, h_dve.at(b, half + 1))
                    if k >= 4:
                        pe.wait_ge((u_act, u_dve)[k % 2].sem, (u_act, u_dve)[k % 2].at(b, (k - 4) // 2 + 1))
                    for c in range(CT):
                        last = nc.tensor.matmul(bank[4 + k % 4][:, :], w1[:, c, o * P:(o + 1) * P],
                                                hT[:, c, half * HALF:(half + 1) * HALF], start=c == 0, stop=c == CT - 1)
                    last.then_inc(u_ps.sem, 1)
                for i in range(NP):
                    if i % (NP // NH) == 0:
                        half = i // (NP // NH)
                        pe.wait_ge(u_act.sem, u_act.at(b, (half + 1) * KT // 2))
                        pe.wait_ge(u_dve.sem, u_dve.at(b, (half + 1) * KT // 2))
                    for t in (2 * i, 2 * i + 1):
                        for c in range(KT):
                            last = nc.tensor.matmul(bank[i][:, (t % 2) * D:(t % 2 + 1) * D],
                                                    uT[:, c, t * P:(t + 1) * P], w2[:, c, :],
                                                    start=c == 0, stop=c == KT - 1)
                    last.then_inc(y3_ps.sem, 1)
                if has_next:
                    project_v(b + 1)

            pe.wait_ge(consts, CONSTS)
            pe.wait_ge(weights_in, 16 * WEIGHT_DMAS)
            transpose_x(0)
            pe.wait_ge(xT_act.sem, xT_act.at(0, 2))
            pe.wait_ge(xT_dve.sem, xT_dve.at(0, 2))
            for k in range(8):
                project(0, k, (wq, wk)[k // 4])
            pe.wait_ge(qk_lo.sem, qk_lo.at(0, 8))
            project_v(0)
            with pe.Fori(0, B - 1) as b:
                batch(b, True)
            batch(B - 1, False)


_INS = ["x", "adj", "L0_gnn_W_q", "L0_gnn_W_k", "L0_gnn_W_v", "L0_gnn_W_e", "L0_gnn_W_o", "L1_gnn_gamma",
        "L1_gnn_beta", "L1_gnn_W_self", "L1_gnn_W_neigh", "L2_gnn_W_rel", "L2_gnn_b_rel", "L2_gnn_W_root",
        "L2_gnn_ln_gamma", "L2_gnn_ln_beta", "L3_gnn_eps", "L3_gnn_W1", "L3_gnn_b1", "L3_gnn_W2", "L3_gnn_b2"]
_TRANSPOSED = ("L0_gnn_W_q", "L0_gnn_W_k", "L0_gnn_W_v", "L0_gnn_W_o")


def kernel(**inputs):
    import numpy as _np
    import concourse.bacc as _bacc
    from concourse import mybir as _mybir
    from concourse.bass_utils import run_bass_kernel_spmd as _run

    nc = _bacc.Bacc("TRN2", target_bir_lowering=False, num_devices=1)
    arrays, args = {}, []
    for name in _INS:
        a = _np.asarray(inputs[name])
        a = _np.ascontiguousarray(a.T if name in _TRANSPOSED else a)
        arrays[f"in_{name}_dram"] = a
        args.append(nc.dram_tensor(f"in_{name}_dram", a.shape, _mybir.dt.from_np(a.dtype), kind="ExternalInput").ap())
    shape = tuple(inputs["x"].shape)
    args.append(nc.dram_tensor("out_0_dram", shape, _mybir.dt.from_np(_np.dtype("float32")), kind="ExternalOutput").ap())
    gnn_stack_kernel(nc, *args)
    r = _run(nc, [arrays], core_ids=[0])
    return r.results[0]["out_0_dram"]
```

```python
from contextlib import ExitStack

import concourse.bass as bass
from concourse import mybir

F32 = mybir.dt.float32
F32R = mybir.dt.float32r
BF16 = mybir.dt.bfloat16
ALU = mybir.AluOpType
ACT = mybir.ActivationFunctionType
AX = mybir.AxisListType

P = 128
LN_EPS = 1e-5
MASKED = -1e30
KB = 1024


class Tally:

    def __init__(self, sem, per_batch, base=0):
        self.sem, self.per_batch, self.base = sem, per_batch, base

    def at(self, b, count):
        return b * self.per_batch + (self.base + count)


def gnn_stack_kernel(nc: bass.Bass, x, adj, W_qT, W_kT, W_vT, W_e, W_oT, L1_gamma, L1_beta, L1_W_self, L1_W_neigh,
                     L2_W_rel, L2_b_rel, L2_W_root, L2_gamma, L2_beta, L3_eps, L3_W1, L3_b1, L3_W2, L3_b2, out):
    B, N, D = x.shape
    H = W_e.shape[0]
    HD = D // H
    HID = L3_W1.shape[1]
    NT = N // P
    CT = D // P
    KT = HID // P
    HALF = 512
    NH = N // HALF
    TPH = HALF // P
    NP = NT // 2
    G = P // HD
    HG = H // G
    UNITS = NT * H
    GROUPS = UNITS // G
    ROW_SLOTS = 5
    PT_SLOTS = 7
    AV_STEPS = ((0, 3), (3, 6), (6, 8))
    EARLY_ADJ = 3
    LAG = 2
    OUT_LAG = LAG + G + len(AV_STEPS)
    SCALE = float(HD) ** -0.5
    assert 2 * D == HALF and G * HD == P and 4 * HD == P

    x_t = x.rearrange("b (t p) d -> b p t d", p=P)
    out_t = out.rearrange("b (t p) d -> b p t d", p=P)
    adj_t = adj.rearrange("b (t p) j -> b p t j", p=P)

    ctx = ExitStack()
    with ctx:
        place = [(nc.sbuf_base + 63) // 64 * 64]

        def at(name, offset, shape, dt):
            return nc.alloc_sbuf_tensor_at(name, shape, dt, offset=offset).ap()

        def sb(name, shape, dt=F32):
            size = 2 if dt == BF16 else 4
            for n in shape[1:]:
                size *= n
            offset = place[0]
            place[0] += (size + 63) // 64 * 64
            return at(name, offset, shape, dt)

        wq = sb("wq", [P, CT, D])
        wk = sb("wk", [P, CT, D])
        wv = sb("wv", [P, CT, D])
        wo = sb("wo", [P, CT, D])
        w_ns = sb("w_ns", [P, CT, 2, D])
        w_rel = sb("w_rel", [P, CT, D])
        w_root = sb("w_root", [P, CT, D])
        w1_hi = sb("w1_hi", [P, CT, HID], F32R)
        w1_lo = sb("w1_lo", [P, CT, HID], F32R)
        w2 = sb("w2", [P, KT, D])
        brel_bc = sb("brel_bc", [P, D])
        b2_bc = sb("b2_bc", [P, D])
        we_bc = sb("we_bc", [P, H])
        eps_bc = sb("eps_bc", [P, 1])
        one_eps = sb("one_eps", [P, 1])
        gam = [sb(f"gam{i}", [P, CT]) for i in range(2)]
        bet = [sb(f"bet{i}", [P, CT]) for i in range(2)]
        b1 = sb("b1", [P, KT])
        ident = sb("ident", [P, P])
        ident_bf = sb("ident_bf", [P, P], BF16)
        diag_eps = sb("diag_eps", [P, P])
        nhalf = sb("nhalf", [P, 2, NT])
        neg_max = sb("neg_max", [P, UNITS])
        row_sum = sb("row_sum", [P, UNITS])
        row_inv = sb("row_inv", [P, UNITS])
        r_bc = sb("r_bc", [P, 2, P])
        bn6 = sb("bn6", [P, NT, 6])
        mv = sb("mv", [P, NT, 2])
        var_e = sb("var_e", [P, 2, NT])
        rstd = sb("rstd", [P, 2, NT])
        mean_root = sb("mean_root", [P, 2, NT])
        neg_mean = sb("neg_mean", [P, 2, NT])
        root2 = sb("root2", [P, NT])
        neg_mean2 = sb("neg_mean2", [P, NT])
        d_part = sb("d_part", [P, 2, NT, NH])
        deg = sb("deg", [P, 2, NT])
        deg0 = sb("deg0", [P, 2, NT])
        deg1 = sb("deg1", [P, 2, NT])
        degp = sb("degp", [P, 2, NT])
        s_deg = sb("s_deg", [P, 2, NT])
        ns_out = sb("ns_out", [P, NT])
        dropped = sb("dropped", [P, HALF], BF16)
        x0 = sb("x0", [P, NT, D])
        rows_at = place[0]
        adj_n = sb("adj_n", [P, NT, N])
        q_hi = at("q_hi", rows_at, [P, CT, N], F32R)
        q_lo = at("q_lo", rows_at + 8 * KB, [P, CT, N], F32R)
        k_hi = at("k_hi", rows_at + 16 * KB, [P, CT, N], F32R)
        k_lo = at("k_lo", rows_at + 24 * KB, [P, CT, N], F32R)
        big = place[0]
        place[0] += 2 * 4 * NT * N
        qs = at("qs", big, [P, H, N], F32R)
        ks = at("ks", big + 32 * KB, [P, H, N], F32R)
        adjT_hi = at("adjT_hi", big, [P, NT, N], F32R)
        adjT_lo = at("adjT_lo", big + 32 * KB, [P, NT, N], F32R)
        m = place[0]
        place[0] += 68 * KB
        assert place[0] <= nc.sbuf_usable_end, place[0]
        pT = at("pT", m, [P, PT_SLOTS, NT, P], F32)
        row = at("row", m + 28 * KB, [P, ROW_SLOTS, N], F32)
        mask = at("mask", m + 48 * KB, [P, 2, N], BF16)
        v_sb = at("v_sb", m + 52 * KB, [P, NT, D], F32)
        oT = at("oT", m + 60 * KB, [P, CT, N], F32)
        res = at("res", m, [P, NT, D], F32)
        cur = at("cur", m + 8 * KB, [P, NT, D], F32)
        xn = at("xn", m + 16 * KB, [P, NT, D], F32)
        xT = at("xT", m + 16 * KB, [P, CT, N], F32)
        nT = at("nT", m + 24 * KB, [P, CT, N], F32)
        hT_hi = at("hT_hi", m + 24 * KB, [P, CT, N], F32R)
        hT_lo = at("hT_lo", m, [P, CT, N], F32R)
        w1_raw = at("w1_raw", m, [P, CT, HID], F32)
        y_out = [at("y_out0", m + 64 * KB, [P, TPH, D], F32), at("y_out1", m + 60 * KB, [P, TPH, D], F32)]
        z_hi = at("z_hi", m + 32 * KB, [P, NT, D], F32R)
        z_lo = at("z_lo", m + 40 * KB, [P, NT, D], F32R)
        pre = at("pre", m + 48 * KB, [P, NT, D], F32)
        soft = at("soft", m + 56 * KB, [P, NT, D], F32)
        x2d = at("x2d", m + 56 * KB, [P, NT, D], F32)
        uT = at("uT", m + 48 * KB, [P, KT, N], F32)

        def late_bank(k):
            return bank[(6, 4, 5, 7)[k % 4]]

        psum = ctx.enter_context(nc.psum_tensor("psum", [P, 8, HALF], F32))
        bank = [psum[:, i, :] for i in range(8)]

        def score_bank(n, half):
            return bank[2 * (n % 2) + half]

        def pT_bank(k):
            return bank[4 + k % 3]

        out_ps = bank[7][:, 0:P]
        rinv_ps = bank[7][:, P:2 * P]

        def score_pair(n):
            return psum[:, 2 * (n % 2):2 * (n % 2) + 2, :].rearrange("p a j -> p (a j)")

        def sem(name):
            return ctx.enter_context(nc.semaphore(name))

        def tally(name, per_batch, base=0):
            return Tally(sem(name), per_batch, base)

        MOVERS = "ADADADAD"

        MASKERS = "PGPPGPPG"

        def pool_masks(n):
            return n // H * MASKERS.count("G") + MASKERS[:n % H].count("G")

        def moves(who, k):
            return k // len(MOVERS) * MOVERS.count(who) + MOVERS[:k % len(MOVERS)].count(who)

        def moved_by(who, k):
            return MOVERS[k % len(MOVERS)] == who

        WEIGHT_DMAS = 16
        CONSTS = 5
        projections_in = sem("projections_in")
        weights_in = sem("weights_in")
        consts = sem("consts")
        pool_passed = sem("pool_passed")
        dve_passed = sem("dve_passed")
        w1_hi_done = sem("w1_hi_done")
        w1_lo_done = sem("w1_lo_done")
        ident_zero = sem("ident_zero")
        ident_done = sem("ident_done")
        x_in = tally("x_in", 16)
        adj_in = [tally(f"adj_in{i}", 16) for i in range(NP)]
        q_stacked = tally("q_stacked", 4 * G * 16)
        k_stacked = tally("k_stacked", 4 * G * 16)
        out_stored = tally("out_stored", 32, base=32)
        xT_ps = tally("xT_ps", 4)
        xT_act = tally("xT_act", 2)
        xT_dve = tally("xT_dve", 2)
        qk_ps = tally("qk_ps", 8)
        qk_hi = tally("qk_hi", 8)
        qk_lo = tally("qk_lo", 8)
        v_ps = tally("v_ps", 4)
        v_act = tally("v_act", 2)
        v_dve = tally("v_dve", 2)
        mask_done = tally("mask_done", NT)
        bias_done = tally("bias_done", UNITS)
        bias_scaled = tally("bias_scaled", NT * MASKERS.count("G"))
        din_done = tally("din_done", NT * NH)
        scores = tally("scores", UNITS)
        logits = tally("logits", UNITS)
        probs = tally("probs", UNITS)
        pT_ps = tally("pT_ps", 2 * UNITS)
        pT_act = tally("pT_act", moves("A", 2 * UNITS))
        pT_dve = tally("pT_dve", moves("D", 2 * UNITS))
        rinv_done = tally("rinv_done", GROUPS)
        av = tally("av", GROUPS)
        r_bc_done = tally("r_bc_done", GROUPS)
        o_norm = tally("o_norm", GROUPS)
        y0_ps = tally("y0_ps", NP)
        adjT_ps = tally("adjT_ps", NT * NH)
        adjT_hi_done = tally("adjT_hi_done", NT * NH)
        adjT_lo_done = tally("adjT_lo_done", NT * NH)
        dout_done = tally("dout_done", 1)
        deg_steps = tally("deg_steps", 5)
        summed = [tally(f"summed{i}", NT if i == 1 else NP, base=NP if i == 3 else 0) for i in range(4)]
        bn_done = [tally(f"bn_done{i}", NT) for i in range(4)]
        mv_done = [tally(f"mv_done{i}", NT) for i in range(4)]
        var_done = [tally(f"var_done{i}", 4 if i < 2 else 2) for i in range(4)]
        rstd_done = [tally(f"rstd_done{i}", 2) for i in range(4)]
        xn_done = [tally(f"xn_done{i}", NT) for i in range(2)]
        x1_done = tally("x1_done", NT)
        x3_done = tally("x3_done", NT)
        nT_ps = [tally(f"nT_ps{i}", 4) for i in range(2)]
        nT_act = [tally(f"nT_act{i}", 2) for i in range(2)]
        nT_dve = [tally(f"nT_dve{i}", 2) for i in range(2)]
        zs_ps = tally("zs_ps", NT)
        self_sb = tally("self_sb", NT)
        z_hi_done = [tally("z_hi_done0", NT), tally("z_hi_done1", NP), tally("z_hi_done2", NP)]
        z_lo_done = [tally("z_lo_done0", NT), tally("z_lo_done1", NP), tally("z_lo_done2", NP)]
        agg_ps = tally("agg_ps", NT)
        pre_done = tally("pre_done", NT)
        abs_done = tally("abs_done", NT)
        exp_done = tally("exp_done", NT)
        ln_done = tally("ln_done", NT)
        relu_done = tally("relu_done", NT)
        z2_ps = tally("z2_ps", NP)
        conv_ps = tally("conv_ps", NP)
        conv_b = tally("conv_b", NP)
        x2d_done = tally("x2d_done", NT)
        shift_steps = [tally(f"shift_steps{i}", 2 * NH) for i in range(2)]
        doubled = tally("doubled", 2 * NH)
        b2_added = tally("b2_added", NT)
        h_ps = tally("h_ps", 4)
        h_hi = tally("h_hi", 4)
        h_lo = tally("h_lo", 4)
        u_ps = tally("u_ps", KT * NH)
        u_act = tally("u_act", KT * NH // 2)
        u_dve = tally("u_dve", KT * NH // 2)
        y3_ps = tally("y3_ps", NP)
        y_done = tally("y_done", NT)

        def rows(t, pair):
            return t[:, 2 * pair:2 * pair + 2, :]

        def half_rows(t, half):
            return t[:, half * TPH:(half + 1) * TPH, :]

        def bank_pair(i):
            return bank[i][:, :].rearrange("p (t d) -> p t d", t=2)

        def over_pair(v):
            return v[:, :].unsqueeze(1).to_broadcast([P, 2, D])

        block = ctx.enter_context(nc.Block())

        @block.sync
        def _(sp):
            def load_projections():
                for dst, src in ((wq, W_qT), (wk, W_kT), (wv, W_vT)):
                    sp.dma_start(dst, src.rearrange("(t p) n -> p t n", p=P)).then_inc(projections_in, 16)

            def load_weights():
                n = 0
                for dst, src in ((wo, W_oT), (w_rel, L2_W_rel), (w_root, L2_W_root), (w1_raw, L3_W1), (w2, L3_W2)):
                    sp.dma_start(dst, src.rearrange("(t p) n -> p t n", p=P)).then_inc(weights_in, 16)
                    n += 1
                for i, src in enumerate((L1_W_neigh, L1_W_self)):
                    sp.dma_start(w_ns[:, :, i, :], src.rearrange("(t p) n -> p t n", p=P)).then_inc(weights_in, 16)
                    n += 1
                for dst, src in ((brel_bc, L2_b_rel), (b2_bc, L3_b2)):
                    sp.dma_start(dst, src.partition_broadcast(P)).then_inc(weights_in, 16)
                    n += 1
                sp.dma_start(we_bc, W_e.rearrange("h o -> (h o)").partition_broadcast(P)).then_inc(weights_in, 16)
                sp.dma_start(eps_bc, L3_eps.partition_broadcast(P)).then_inc(weights_in, 16)
                n += 2
                with nc.allow_non_contiguous_dma("per-partition vectors of a few hundred values"):
                    for dst, src in ((gam[0], L1_gamma), (bet[0], L1_beta), (gam[1], L2_gamma), (bet[1], L2_beta),
                                     (b1, L3_b1)):
                        sp.dma_start(dst, src.rearrange("(t p) -> p t", p=P)).then_inc(weights_in, 16)
                        n += 1
                assert n == WEIGHT_DMAS

            def load_x(b):
                sp.dma_start(x0, x_t[b]).then_inc(x_in.sem, 16)

            def stack(b, first, dst, parts, stacked):
                sp.wait_ge(qk_hi.sem, qk_hi.at(b, first + 4))
                sp.wait_ge(qk_lo.sem, qk_lo.at(b, first + 4))
                for r in range(G):
                    for part, src in enumerate(parts):
                        sp.dma_start(dst[HD * part:HD * (part + 1), r::G, :].bitcast(F32),
                                     src[HD * r:HD * (r + 1), :, :].bitcast(F32)).then_inc(stacked.sem, 16)

            def enter_batch(b):
                stack(b, 0, qs, (q_hi, q_hi, q_lo, q_lo), q_stacked)
                stack(b, 4, ks, (k_hi, k_lo, k_hi, k_lo), k_stacked)
                for i in range(NP):
                    if i == 0:
                        sp.wait_ge(q_stacked.sem, q_stacked.at(b, 4 * G * 16))
                    if i == NP // 2:
                        sp.wait_ge(k_stacked.sem, k_stacked.at(b, 4 * G * 16))
                    sp.dma_start(rows(adj_n, i), adj_t[b][:, 2 * i:2 * i + 2, :]).then_inc(adj_in[i].sem, 16)

            def leave_batch(b, has_next):
                if has_next:
                    sp.wait_ge(summed[0].sem, summed[0].at(b, NP))
                    load_x(b + 1)
                    sp.wait_ge(h_ps.sem, h_ps.at(b, 4))
                    enter_batch(b + 1)
                for half in range(NH):
                    sp.wait_ge(y_done.sem, y_done.at(b, TPH * (half + 1)))
                    ts = slice(half * TPH, (half + 1) * TPH)
                    sp.dma_start(out_t[b][:, ts, :], y_out[half]).then_inc(out_stored.sem, 16)

            load_x(0)
            load_projections()
            load_weights()
            enter_batch(0)
            with sp.Fori(0, B - 1) as b:
                leave_batch(b, True)
            leave_batch(B - 1, False)
            sp.wait_ge(out_stored.sem, out_stored.at(B - 1, 32))

        @block.gpsimd
        def _(pool):
            nc.gpsimd.memset(ident, 0.0).then_inc(ident_zero, 1)
            pool.wait_ge(ident_zero, 1)
            nc.gpsimd.affine_select(out=ident, in_=ident, compare_op=ALU.not_equal, fill=1.0, base=0,
                                    pattern=[[-1, P]], channel_multiplier=1).then_inc(ident_done, 1)
            pool.wait_ge(ident_done, 1)
            nc.gpsimd.tensor_copy(ident_bf, ident).then_inc(consts, 1)
            nc.gpsimd.memset(nhalf, -0.5).then_inc(consts, 1)
            pool.wait_ge(weights_in, 16 * WEIGHT_DMAS)
            nc.gpsimd.tensor_tensor(w_ns[:, :, 1, :], w_ns[:, :, 1, :], w_ns[:, :, 0, :], ALU.add).then_inc(consts, 1)
            nc.gpsimd.tensor_scalar(one_eps, eps_bc, 1.0, 1.0, ALU.mult, ALU.add).then_inc(consts, 1)
            pool.wait_ge(consts, 4)
            nc.gpsimd.tensor_scalar(diag_eps, ident, one_eps[:, 0:1], 0.0, ALU.mult, ALU.add).then_inc(consts, 1)

            def norm_root(b, l, half):
                kinds = 2 if l < 2 else 1
                ts = slice(half * TPH, (half + 1) * TPH)
                pool.wait_ge(mv_done[l].sem, mv_done[l].at(b, TPH * (half + 1)))
                pool.sem_inc(pool_passed)
                nc.gpsimd.tensor_scalar(var_e[:, 0, ts], mv[:, ts, 1], 1.0, LN_EPS, ALU.mult, ALU.add)\
                    .then_inc(var_done[l].sem, 1)
                if kinds == 2:
                    nc.gpsimd.tensor_scalar(var_e[:, 1, ts], mv[:, ts, 1], 1.0 + LN_EPS, LN_EPS * LN_EPS, ALU.mult,
                                            ALU.add).then_inc(var_done[l].sem, 1)
                pool.wait_ge(var_done[l].sem, var_done[l].at(b, kinds * (half + 1)))
                nc.gpsimd.tensor_tensor(rstd[:, 0:kinds, ts], var_e[:, 0:kinds, ts], nhalf[:, 0:kinds, ts], ALU.pow)\
                    .then_inc(rstd_done[l].sem, 1)

            def norm_shift(b, l, half):
                ts = slice(half * TPH, (half + 1) * TPH)
                pool.wait_ge(rstd_done[l].sem, rstd_done[l].at(b, half + 1))
                nc.gpsimd.tensor_tensor(mean_root[:, :, ts], mv[:, ts, 0:1].rearrange("p t o -> p o t")
                                        .to_broadcast([P, 2, TPH]), rstd[:, :, ts], ALU.mult)\
                    .then_inc(shift_steps[l].sem, 1)
                pool.wait_ge(shift_steps[l].sem, shift_steps[l].at(b, 2 * half + 1))
                pool.sem_inc(pool_passed)
                nc.gpsimd.tensor_scalar(neg_mean[:, :, ts], mean_root[:, :, ts], -1.0, 0.0, ALU.mult, ALU.add)\
                    .then_inc(shift_steps[l].sem, 1)

            with pool.Fori(0, B) as b:
                for n in range(UNITS):
                    t, h = n // H, n % H
                    if h == 0 and t % 2 == 0:
                        pool.wait_ge(adj_in[t // 2].sem, adj_in[t // 2].at(b, 16))
                        pool.sem_inc(pool_passed)
                    if n >= ROW_SLOTS:
                        pool.wait_ge(pT_ps.sem, pT_ps.at(b, 2 * (n - ROW_SLOTS) + 2))
                        pool.sem_inc(pool_passed)
                    slot = row[:, n % ROW_SLOTS, :]
                    nc.gpsimd.tensor_scalar(slot, adj_n[:, t, :], we_bc[:, h:h + 1], 0.0, ALU.mult, ALU.add)\
                        .then_inc((bias_scaled if MASKERS[h] == "G" else bias_done).sem, 1)
                    if MASKERS[h] == "G":
                        pool.wait_ge(bias_scaled.sem, bias_scaled.at(b, pool_masks(n + 1)))
                        pool.wait_ge(mask_done.sem, mask_done.at(b, t + 1))
                        nc.gpsimd.tensor_tensor(slot, slot, mask[:, t % 2, :], ALU.add).then_inc(bias_done.sem, 1)
                for half in range(NH):
                    norm_root(b, 0, half)
                    norm_shift(b, 0, half)
                pool.wait_ge(shift_steps[0].sem, shift_steps[0].at(b, 2 * NH))
                pool.sem_inc(pool_passed)
                for t in range(NT):
                    nc.gpsimd.tensor_scalar(cur[:, t, :], res[:, t, :], rstd[:, 0, t:t + 1], neg_mean[:, 0, t:t + 1],
                                            ALU.mult, ALU.add).then_inc(x1_done.sem, 1)
                pool.wait_ge(dout_done.sem, dout_done.at(b, 1))
                pool.sem_inc(pool_passed)
                nc.gpsimd.tensor_scalar(deg0, deg, 0.0, 1.0, ALU.is_equal, ALU.mult).then_inc(deg_steps.sem, 1)
                pool.wait_ge(deg_steps.sem, deg_steps.at(b, 1))
                nc.gpsimd.tensor_tensor(deg1, deg, deg0, ALU.add).then_inc(deg_steps.sem, 1)
                pool.wait_ge(deg_steps.sem, deg_steps.at(b, 2))
                nc.gpsimd.tensor_tensor(degp, deg1, nhalf, ALU.pow).then_inc(deg_steps.sem, 1)
                pool.wait_ge(deg_steps.sem, deg_steps.at(b, 3))
                nc.gpsimd.tensor_tensor(s_deg, degp, deg0, ALU.subtract).then_inc(deg_steps.sem, 1)
                pool.wait_ge(deg_steps.sem, deg_steps.at(b, 4))
                pool.sem_inc(pool_passed)
                nc.gpsimd.tensor_scalar(ns_out, s_deg[:, 1, :], -1.0, 0.0, ALU.mult, ALU.add).then_inc(deg_steps.sem, 1)
                for half in range(NH):
                    norm_root(b, 1, half)
                for half in range(NH):
                    norm_shift(b, 1, half)
                    ts = slice(half * TPH, (half + 1) * TPH)
                    pool.wait_ge(shift_steps[1].sem, shift_steps[1].at(b, 2 * (half + 1)))
                    pool.sem_inc(pool_passed)
                    nc.gpsimd.tensor_scalar(root2[:, ts], rstd[:, 0, ts], 2.0, 0.0, ALU.mult, ALU.add)\
                        .then_inc(doubled.sem, 1)
                    nc.gpsimd.tensor_scalar(neg_mean2[:, ts], neg_mean[:, 0, ts], 2.0, 0.0, ALU.mult, ALU.add)\
                        .then_inc(doubled.sem, 1)
                    pool.wait_ge(doubled.sem, doubled.at(b, 2 * (half + 1)))
                    pool.sem_inc(pool_passed)
                    for t in range(half * TPH, (half + 1) * TPH):
                        nc.gpsimd.tensor_scalar(x2d[:, t, :], res[:, t, :], root2[:, t:t + 1], neg_mean2[:, t:t + 1],
                                                ALU.mult, ALU.add).then_inc(x2d_done.sem, 1)
                for half in range(NH):
                    norm_root(b, 2, half)
                pool.wait_ge(h_ps.sem, h_ps.at(b, 4))
                for t in range(NT):
                    nc.gpsimd.tensor_tensor(cur[:, t, :], cur[:, t, :], b2_bc, ALU.add).then_inc(b2_added.sem, 1)
                for half in range(NH):
                    norm_root(b, 3, half)

        @block.scalar
        def _(act):
            nc.scalar.preload_act_table_set("natural_log_exp_and_others")

            def transpose_x(b):
                for k in (0, 2):
                    act.wait_ge(xT_ps.sem, xT_ps.at(b, k + 1))
                    nc.scalar.activation(xT[:, k % CT, (k // CT) * HALF:(k // CT + 1) * HALF], bank[k], ACT.Copy)\
                        .then_inc(xT_act.sem, 1)

            def project(b, first, hi, scale):
                for k in range(4):
                    act.wait_ge(qk_ps.sem, qk_ps.at(b, first + k + 1))
                    nc.scalar.activation(hi[:, k // 2, (k % 2) * HALF:(k % 2 + 1) * HALF], bank[first + k], ACT.Copy,
                                         scale=scale).then_inc(qk_hi.sem, 1)

            def project_v(b):
                for k in (0, 2):
                    act.wait_ge(v_ps.sem, v_ps.at(b, k + 1))
                    nc.scalar.activation(rows(v_sb, k), bank_pair(4 + k), ACT.Copy).then_inc(v_act.sem, 1)

            def batch(b, has_next):
                def adjT_high(k):
                    act.wait_ge(adjT_ps.sem, adjT_ps.at(b, k + 1))
                    half, j = k // NT, k % NT
                    nc.scalar.activation(adjT_hi[:, j, half * HALF:(half + 1) * HALF], late_bank(k),
                                         ACT.Identity, accum_out=d_part[:, 1, j, half:half + 1])\
                        .then_inc(adjT_hi_done.sem, 1)

                for n in range(UNITS + OUT_LAG - G + 1):
                    if 1 <= n <= UNITS:
                        u = n - 1
                        act.wait_ge(logits.sem, logits.at(b, u + 1))
                        nc.scalar.activation(row[:, u % ROW_SLOTS, :], row[:, u % ROW_SLOTS, :], ACT.Exp, scale=-1.0,
                                             bias=neg_max[:, u:u + 1], accum_out=row_sum[:, u:u + 1])\
                            .then_inc(probs.sem, 1)
                    if LAG <= n < UNITS + LAG:
                        u = n - LAG
                        if u >= PT_SLOTS:
                            act.wait_ge(av.sem, av.at(b, (u - PT_SLOTS) // G + 1))
                        for k in (2 * u, 2 * u + 1):
                            if moved_by("A", k):
                                act.wait_ge(pT_ps.sem, pT_ps.at(b, k + 1))
                                nc.scalar.activation(pT[:, u % PT_SLOTS, k % 2 * TPH:(k % 2 + 1) * TPH, :],
                                                     pT_bank(k).rearrange("p (j i) -> p j i", j=TPH), ACT.Copy)\
                                    .then_inc(pT_act.sem, 1)
                    if n % H == H - 2 and n < UNITS:
                        t = n // H
                        if t % 2 == 0:
                            act.wait_ge(adj_in[t // 2].sem, adj_in[t // 2].at(b, 16))
                        for half in range(NH):
                            if t >= 1 or half == 1:
                                act.wait_ge(din_done.sem, din_done.at(b, NH * t + half))
                            nc.scalar.activation(dropped, adj_n[:, t, half * HALF:(half + 1) * HALF], ACT.Copy,
                                                 accum_out=d_part[:, 0, t, half:half + 1]).then_inc(din_done.sem, 1)
                    if 0 <= n - UNITS - LAG < EARLY_ADJ:
                        adjT_high(n - UNITS - LAG)
                    if n >= OUT_LAG and (n - OUT_LAG) % G == 0 and (n - OUT_LAG) // G < GROUPS:
                        g = (n - OUT_LAG) // G
                        act.wait_ge(av.sem, av.at(b, g + 1))
                        nc.scalar.activation(r_bc[:, g % 2, :], rinv_ps, ACT.Copy)\
                            .then_inc(r_bc_done.sem, 1)

                def normalise(half):
                    act.wait_ge(shift_steps[0].sem, shift_steps[0].at(b, 2 * (half + 1)))
                    for t in range(half * TPH, (half + 1) * TPH):
                        nc.scalar.activation(xn[:, t, :], res[:, t, :], ACT.Identity, scale=rstd[:, 1, t:t + 1],
                                             bias=neg_mean[:, 1, t:t + 1]).then_inc(xn_done[0].sem, 1)

                for k in range(EARLY_ADJ, NT * NH):
                    adjT_high(k)
                    if k == NT:
                        normalise(0)
                normalise(1)

                def norm_transposed(l, half, first):
                    k = CT * half
                    act.wait_ge(nT_ps[l].sem, nT_ps[l].at(b, k + 1))
                    nc.scalar.activation(nT[:, 0, half * HALF:(half + 1) * HALF], bank[first + k], ACT.Identity,
                                         scale=gam[l][:, 0:1], bias=bet[l][:, 0:1]).then_inc(nT_act[l].sem, 1)

                for half in range(NH):
                    norm_transposed(0, half, 0)
                for t in range(NT):
                    act.wait_ge(zs_ps.sem, zs_ps.at(b, t + 1))
                    nc.scalar.activation(pre[:, t, :], late_bank(t)[:, D:2 * D], ACT.Copy).then_inc(self_sb.sem, 1)
                    if t == 0:
                        act.wait_ge(deg_steps.sem, deg_steps.at(b, 4))
                    nc.scalar.activation(z_hi[:, t, :], late_bank(t)[:, 0:D], ACT.Copy, scale=s_deg[:, 0, t:t + 1])\
                        .then_inc(z_hi_done[0].sem, 1)
                for t in range(NT):
                    act.wait_ge(pre_done.sem, pre_done.at(b, t + 1))
                    nc.scalar.activation(soft[:, t, :], pre[:, t, :], ACT.Abs).then_inc(abs_done.sem, 1)
                    act.wait_ge(abs_done.sem, abs_done.at(b, t + 1))
                    nc.scalar.activation(soft[:, t, :], soft[:, t, :], ACT.Exp, scale=-1.0).then_inc(exp_done.sem, 1)
                    act.wait_ge(exp_done.sem, exp_done.at(b, t + 1))
                    nc.scalar.activation(soft[:, t, :], soft[:, t, :], ACT.Ln, bias=1.0).then_inc(ln_done.sem, 1)
                    if t == NT - 2:
                        norm_transposed(1, 0, 4)
                for half in range(NH):
                    if half == 1:
                        norm_transposed(1, 1, 4)
                    for i in range(half * NP // NH, (half + 1) * NP // NH):
                        act.wait_ge(z2_ps.sem, z2_ps.at(b, i + 1))
                        nc.scalar.activation(rows(z_hi, i), bank_pair(i), ACT.Copy).then_inc(z_hi_done[1].sem, 1)
                if has_next:
                    transpose_x(b + 1)
                    project(b + 1, 0, q_hi, SCALE)
                act.wait_ge(conv_ps.sem, conv_ps.at(b, NP))
                for i in range(NP):
                    act.wait_ge(x3_done.sem, x3_done.at(b, 2 * i + 2))
                    nc.scalar.activation(rows(z_hi, i), rows(cur, i), ACT.Copy).then_inc(z_hi_done[2].sem, 1)
                if has_next:
                    project(b + 1, 4, k_hi, 1.0)
                for k in range(CT * NH):
                    act.wait_ge(h_ps.sem, h_ps.at(b, k + 1))
                    nc.scalar.activation(hT_hi[:, k % 2, (k // 2) * HALF:(k // 2 + 1) * HALF], bank[k], ACT.Copy)\
                        .then_inc(h_hi.sem, 1)
                for k in range(0, KT * NH, 2):
                    act.wait_ge(u_ps.sem, u_ps.at(b, k + 1))
                    nc.scalar.activation(uT[:, k % KT, (k // KT) * HALF:(k // KT + 1) * HALF], bank[4 + k % 4][:, :],
                                         ACT.Relu, bias=b1[:, k % KT:k % KT + 1]).then_inc(u_act.sem, 1)
                if has_next:
                    project_v(b + 1)

            transpose_x(0)
            project(0, 0, q_hi, SCALE)
            project(0, 4, k_hi, 1.0)
            project_v(0)
            act.wait_ge(weights_in, 16 * WEIGHT_DMAS)
            nc.scalar.activation(w1_hi, w1_raw, ACT.Copy).then_inc(w1_hi_done, 1)
            with act.Fori(0, B - 1) as b:
                batch(b, True)
            batch(B - 1, False)

        @block.vector
        def _(dve):
            nc.vector.memset(row_sum, 0.0).then_inc(summed[3].sem, NP)
            nc.vector.memset(row_inv, 0.0).then_inc(out_stored.sem, 32)

            def transpose_x(b):
                for k in (1, 3):
                    dve.wait_ge(xT_ps.sem, xT_ps.at(b, k + 1))
                    nc.vector.tensor_copy(xT[:, k % CT, (k // CT) * HALF:(k // CT + 1) * HALF], bank[k])\
                        .then_inc(xT_dve.sem, 1)

            def project(b, first, hi, lo, scale):
                for k in range(4):
                    dve.wait_ge(qk_hi.sem, qk_hi.at(b, first + k + 1))
                    cols = slice((k % 2) * HALF, (k % 2 + 1) * HALF)
                    nc.vector.scalar_tensor_tensor(lo[:, k // 2, cols], bank[first + k], scale,
                                                   hi[:, k // 2, cols].bitcast(F32), ALU.mult, ALU.subtract)\
                        .then_inc(qk_lo.sem, 1)

            def project_v(b):
                for k in (1, 3):
                    dve.wait_ge(v_ps.sem, v_ps.at(b, k + 1))
                    nc.vector.tensor_copy(rows(v_sb, k), bank_pair(4 + k)).then_inc(v_dve.sem, 1)

            def make_mask(b, t):
                if t % 2 == 0:
                    dve.wait_ge(adj_in[t // 2].sem, adj_in[t // 2].at(b, 16))
                nc.vector.tensor_scalar(mask[:, t % 2, :], adj_n[:, t, :], 0.0, MASKED, ALU.is_equal, ALU.mult)\
                    .then_inc(mask_done.sem, 1)

            def batch(b, has_next):
                def adjT_low(k):
                    dve.wait_ge(adjT_hi_done.sem, adjT_hi_done.at(b, k + 1))
                    half, j = k // NT, k % NT
                    cols = slice(half * HALF, (half + 1) * HALF)
                    nc.vector.tensor_tensor(adjT_lo[:, j, cols], late_bank(k),
                                            adjT_hi[:, j, cols].bitcast(F32), ALU.subtract)\
                        .then_inc(adjT_lo_done.sem, 1)

                for n in range(UNITS + OUT_LAG - G + 1):
                    if n < UNITS:
                        dve.wait_ge(bias_done.sem, bias_done.at(b, n + 1))
                        dve.wait_ge(scores.sem, scores.at(b, n + 1))
                        dve.sem_inc(dve_passed)
                        slot = row[:, n % ROW_SLOTS, :]
                        nc.vector.tensor_tensor_reduce(slot, score_pair(n), slot, -1.0, 3e38, ALU.add, ALU.min,
                                                       neg_max[:, n:n + 1])\
                            .then_inc(logits.sem, 1)
                    if n % H == 3 and n // H + 1 < NT:
                        make_mask(b, n // H + 1)
                    if LAG <= n < UNITS + LAG:
                        u = n - LAG
                        if u >= PT_SLOTS:
                            dve.wait_ge(av.sem, av.at(b, (u - PT_SLOTS) // G + 1))
                        for k in (2 * u, 2 * u + 1):
                            if moved_by("D", k):
                                dve.wait_ge(pT_ps.sem, pT_ps.at(b, k + 1))
                                nc.vector.tensor_copy(pT[:, u % PT_SLOTS, k % 2 * TPH:(k % 2 + 1) * TPH, :],
                                                      pT_bank(k).rearrange("p (j i) -> p j i", j=TPH))\
                                    .then_inc(pT_dve.sem, 1)
                    if n >= G + 1 and (n - G - 1) % G == 0 and (n - G - 1) // G < GROUPS:
                        g = (n - G - 1) // G
                        dve.wait_ge(probs.sem, probs.at(b, G * g + G))
                        nc.vector.reciprocal(row_inv[:, G * g:G * g + G], row_sum[:, G * g:G * g + G])\
                            .then_inc(rinv_done.sem, 1)
                    if 0 <= n - UNITS - LAG < EARLY_ADJ:
                        adjT_low(n - UNITS - LAG)
                    if n >= OUT_LAG and (n - OUT_LAG) % G == 0 and (n - OUT_LAG) // G < GROUPS:
                        g = (n - OUT_LAG) // G
                        dve.wait_ge(r_bc_done.sem, r_bc_done.at(b, g + 1))
                        t, hg = g // HG, g % HG
                        if g == 0:
                            dve.wait_ge(out_stored.sem, out_stored.at(b, 0))
                        nc.vector.tensor_tensor(oT[:, hg, t * P:(t + 1) * P], out_ps,
                                                r_bc[:, g % 2, :], ALU.mult).then_inc(o_norm.sem, 1)

                def row_stats(l, i, ts=None):
                    dve.wait_ge(summed[l].sem, summed[l].at(b, i + 1))
                    for t in ts or (2 * i, 2 * i + 1):
                        nc.vector.bn_stats(bn6[:, t, :], res[:, t, :]).then_inc(bn_done[l].sem, 1)

                def row_moments(l, half):
                    dve.wait_ge(bn_done[l].sem, bn_done[l].at(b, TPH * (half + 1)))
                    dve.sem_inc(dve_passed)
                    for t in range(half * TPH, (half + 1) * TPH):
                        nc.vector.bn_aggr(mv[:, t, :], bn6[:, t, :]).then_inc(mv_done[l].sem, 1)

                def normalise(l, half, kind, dst, done):
                    dve.wait_ge(rstd_done[l].sem, rstd_done[l].at(b, half + 1))
                    for i in range(TPH):
                        t = half * TPH + i
                        nc.vector.tensor_scalar(dst[:, i, :], res[:, t, :], mv[:, t, 0:1], rstd[:, kind, t:t + 1],
                                                ALU.subtract, ALU.mult).then_inc(done.sem, 1)

                def norm_transposed(l, half, first):
                    k = CT * half + 1
                    dve.wait_ge(nT_ps[l].sem, nT_ps[l].at(b, k + 1))
                    nc.vector.tensor_scalar(nT[:, 1, half * HALF:(half + 1) * HALF], bank[first + k],
                                            gam[l][:, 1:2], bet[l][:, 1:2], ALU.mult, ALU.add)\
                        .then_inc(nT_dve[l].sem, 1)

                for i in range(NP):
                    dve.wait_ge(y0_ps.sem, y0_ps.at(b, i + 1))
                    nc.vector.tensor_tensor(rows(res, i), bank_pair(i), rows(x0, i), ALU.add).then_inc(summed[0].sem, 1)
                    row_stats(0, i)
                    if i % 2:
                        row_moments(0, i // 2)
                    if i < NP - 1:
                        for k in (3 + 2 * i, 4 + 2 * i):
                            adjT_low(k)
                for k in range(9, 15):
                    adjT_low(k)
                norm_transposed(0, 0, 0)
                adjT_low(15)
                dve.wait_ge(din_done.sem, din_done.at(b, NT * NH))
                nc.vector.tensor_tensor(deg, d_part[:, :, :, 0], d_part[:, :, :, 1], ALU.add)\
                    .then_inc(dout_done.sem, 1)
                norm_transposed(0, 1, 0)
                for t in range(NT):
                    dve.wait_ge(z_hi_done[0].sem, z_hi_done[0].at(b, t + 1))
                    nc.vector.scalar_tensor_tensor(z_lo[:, t, :], late_bank(t)[:, 0:D], s_deg[:, 0, t:t + 1],
                                                   z_hi[:, t, :].bitcast(F32), ALU.mult, ALU.subtract)\
                        .then_inc(z_lo_done[0].sem, 1)
                dve.wait_ge(deg_steps.sem, deg_steps.at(b, 5))
                dve.wait_ge(x1_done.sem, x1_done.at(b, NT))

                def add_softplus(t):
                    dve.wait_ge(relu_done.sem, relu_done.at(b, t + 1))
                    dve.wait_ge(ln_done.sem, ln_done.at(b, t + 1))
                    nc.vector.tensor_tensor(res[:, t, :], pre[:, t, :], soft[:, t, :], ALU.add)\
                        .then_inc(summed[1].sem, 1)
                    row_stats(1, t, (t,))

                for t in range(NT):
                    dve.wait_ge(agg_ps.sem, agg_ps.at(b, t + 1))
                    nc.vector.scalar_tensor_tensor(pre[:, t, :], bank[t % 4][:, 0:D], ns_out[:, t:t + 1], pre[:, t, :],
                                                   ALU.mult, ALU.add).then_inc(pre_done.sem, 1)
                    if t >= 1:
                        add_softplus(t - 1)
                    if t == TPH:
                        row_moments(1, 0)
                    if t == TPH + 1:
                        normalise(1, 0, 1, half_rows(xn, 0), xn_done[1])
                    dve.wait_ge(pre_done.sem, pre_done.at(b, t + 1))
                    dve.wait_ge(abs_done.sem, abs_done.at(b, t + 1))
                    nc.vector.scalar_tensor_tensor(pre[:, t, :], pre[:, t, :], 0.0, cur[:, t, :], ALU.max, ALU.add)\
                        .then_inc(relu_done.sem, 1)
                    if t == NT - 2:
                        norm_transposed(1, 0, 4)
                add_softplus(NT - 1)
                row_moments(1, 1)

                def z2_low(i):
                    dve.wait_ge(z_hi_done[1].sem, z_hi_done[1].at(b, i + 1))
                    nc.vector.tensor_tensor(rows(z_lo, i), bank_pair(i), rows(z_hi, i).bitcast(F32), ALU.subtract)\
                        .then_inc(z_lo_done[1].sem, 1)

                z2_low(0)
                normalise(1, 1, 1, half_rows(xn, 1), xn_done[1])
                z2_low(1)
                norm_transposed(1, 1, 4)
                for i in range(NP // NH, NP):
                    z2_low(i)
                if has_next:
                    transpose_x(b + 1)
                for i in range(NP):
                    dve.wait_ge(conv_ps.sem, conv_ps.at(b, i + 1))
                    nc.vector.tensor_tensor(rows(pre, i), bank_pair(4 + i), over_pair(brel_bc), ALU.add)\
                        .then_inc(conv_b.sem, 1)
                    dve.wait_ge(conv_b.sem, conv_b.at(b, i + 1))
                    dve.wait_ge(x2d_done.sem, x2d_done.at(b, 2 * i + 2))
                    nc.vector.scalar_tensor_tensor(rows(res, i), rows(pre, i), 0.0, rows(x2d, i), ALU.max, ALU.add)\
                        .then_inc(summed[2].sem, 1)
                    row_stats(2, i)
                    if i % 2:
                        row_moments(2, i // 2)
                        normalise(2, i // 2, 0, half_rows(cur, i // 2), x3_done)
                if has_next:
                    project(b + 1, 0, q_hi, q_lo, SCALE)
                for i in range(NP):
                    dve.wait_ge(z_hi_done[2].sem, z_hi_done[2].at(b, i + 1))
                    nc.vector.tensor_tensor(rows(z_lo, i), rows(cur, i), rows(z_hi, i).bitcast(F32), ALU.subtract)\
                        .then_inc(z_lo_done[2].sem, 1)
                if has_next:
                    project(b + 1, 4, k_hi, k_lo, 1.0)
                for k in range(CT * NH):
                    dve.wait_ge(h_hi.sem, h_hi.at(b, k + 1))
                    cols = slice((k // 2) * HALF, (k // 2 + 1) * HALF)
                    nc.vector.tensor_tensor(hT_lo[:, k % 2, cols], bank[k], hT_hi[:, k % 2, cols].bitcast(F32),
                                            ALU.subtract).then_inc(h_lo.sem, 1)
                for k in range(1, KT * NH, 2):
                    dve.wait_ge(u_ps.sem, u_ps.at(b, k + 1))
                    nc.vector.tensor_scalar(uT[:, k % KT, (k // KT) * HALF:(k // KT + 1) * HALF], bank[4 + k % 4],
                                            b1[:, k % KT:k % KT + 1], 0.0, ALU.add, ALU.max).then_inc(u_dve.sem, 1)
                for i in range(NP):
                    dve.wait_ge(b2_added.sem, b2_added.at(b, 2 * i + 2))
                    dve.wait_ge(y3_ps.sem, y3_ps.at(b, i + 1))
                    nc.vector.tensor_tensor(rows(res, i), bank_pair(i), rows(cur, i), ALU.add)\
                        .then_inc(summed[3].sem, 1)
                    row_stats(3, i)
                    if i % 2:
                        row_moments(3, i // 2)
                        if has_next and i == NP - 1:
                            make_mask(b + 1, 0)
                        normalise(3, i // 2, 0, y_out[i // 2], y_done)
                if has_next:
                    project_v(b + 1)

            transpose_x(0)
            project(0, 0, q_hi, q_lo, SCALE)
            project(0, 4, k_hi, k_lo, 1.0)
            project_v(0)
            make_mask(0, 0)
            dve.wait_ge(weights_in, 16 * WEIGHT_DMAS)
            dve.wait_ge(w1_hi_done, 1)
            nc.vector.tensor_tensor(w1_lo, w1_raw, w1_hi.bitcast(F32), ALU.subtract).then_inc(w1_lo_done, 1)
            with dve.Fori(0, B - 1) as b:
                batch(b, True)
            batch(B - 1, False)

        @block.tensor
        def _(pe):
            def split_product(dst, lhs_hi, lhs_lo, rhs_hi, rhs_lo, start, stop):
                nc.tensor.matmul(dst, lhs_hi, rhs_lo, start=start, stop=False)
                nc.tensor.matmul(dst, lhs_hi, rhs_hi, start=False, stop=False)
                return nc.tensor.matmul(dst, lhs_lo, rhs_hi, start=False, stop=stop)

            def rows_transposed(src, half, first, done):
                for c in range(CT):
                    for j in range(TPH):
                        last = nc.tensor.transpose(bank[first + half * CT + c][:, j * P:(j + 1) * P],
                                                   src[:, half * TPH + j, c * P:(c + 1) * P], ident)
                    last.then_inc(done.sem, 1)

            def transpose_x(b):
                pe.wait_ge(x_in.sem, x_in.at(b, 16))
                for half in range(NH):
                    rows_transposed(x0, half, 0, xT_ps)

            def project(b, k, w):
                for c in range(CT):
                    last = nc.tensor.matmul(bank[k], w[:, c, k % 4 // 2 * P:(k % 4 // 2 + 1) * P],
                                            xT[:, c, k % 2 * HALF:(k % 2 + 1) * HALF], start=c == 0, stop=c == CT - 1)
                last.then_inc(qk_ps.sem, 1)

            def project_v(b):
                for i in range(NP):
                    for t in (2 * i, 2 * i + 1):
                        for c in range(CT):
                            last = nc.tensor.matmul(bank[4 + i][:, (t % 2) * D:(t % 2 + 1) * D],
                                                    xT[:, c, t * P:(t + 1) * P], wv[:, c, :],
                                                    start=c == 0, stop=c == CT - 1)
                    last.then_inc(v_ps.sem, 1)

            def batch(b, has_next):
                pe.wait_ge(q_stacked.sem, q_stacked.at(b, 4 * G * 16))
                pe.wait_ge(k_stacked.sem, k_stacked.at(b, 4 * G * 16))
                pe.wait_ge(summed[3].sem, summed[3].at(b, 0))

                def transpose_adj(k):
                    half, j = k // NT, k % NT
                    if k == 3:
                        pe.wait_ge(o_norm.sem, o_norm.at(b, GROUPS))
                    elif k < EARLY_ADJ:
                        pe.wait_ge(pT_act.sem, pT_act.at(b, moves("A", 2 * UNITS - 2 + k)))
                        pe.wait_ge(pT_dve.sem, pT_dve.at(b, moves("D", 2 * UNITS - 2 + k)))
                    if k >= 4:
                        pe.wait_ge(adjT_lo_done.sem, adjT_lo_done.at(b, k - 3))
                    for i in range(TPH):
                        last = nc.tensor.transpose(late_bank(k)[:, i * P:(i + 1) * P],
                                                   adj_n[:, half * TPH + i, j * P:(j + 1) * P], ident)
                    last.then_inc(adjT_ps.sem, 1)

                for n in range(UNITS + LAG + len(AV_STEPS)):
                    if n < UNITS:
                        t, h = n // H, n % H
                        if n >= 2:
                            pe.wait_ge(logits.sem, logits.at(b, n - 1))
                        if h == 0:
                            pe.wait_ge(mask_done.sem, mask_done.at(b, t + 1))
                        masks = MASKERS[h] == "P"
                        for half in range(NH):
                            cols = slice(half * HALF, (half + 1) * HALF)
                            if masks:
                                nc.tensor.matmul(score_bank(n, half), ident_bf, mask[:, t % 2, cols],
                                                 start=True, stop=False)
                            last = nc.tensor.matmul(score_bank(n, half), qs[:, h, t * P:(t + 1) * P],
                                                    ks[:, h, cols], start=not masks, stop=True)
                        last.then_inc(scores.sem, 1)
                    if n == LAG:
                        pe.wait_ge(v_act.sem, v_act.at(b, 2))
                        pe.wait_ge(v_dve.sem, v_dve.at(b, 2))
                    if LAG <= n < UNITS + LAG:
                        u = n - LAG
                        pe.wait_ge(probs.sem, probs.at(b, u + 1))
                        for k in (2 * u, 2 * u + 1):
                            if k >= 3 and moved_by("A", k - 3):
                                pe.wait_ge(pT_act.sem, pT_act.at(b, moves("A", k - 2)))
                            if k >= 3 and moved_by("D", k - 3):
                                pe.wait_ge(pT_dve.sem, pT_dve.at(b, moves("D", k - 2)))
                            for i in range(TPH):
                                j = k % 2 * TPH + i
                                last = nc.tensor.transpose(pT_bank(k)[:, i * P:(i + 1) * P],
                                                           row[:, u % ROW_SLOTS, j * P:(j + 1) * P], ident)
                            last.then_inc(pT_ps.sem, 1)
                    if 0 <= n - UNITS - LAG < EARLY_ADJ:
                        transpose_adj(n - UNITS - LAG)
                    g, step = (n - LAG - G) // G, (n - LAG) % G
                    if 0 <= g < GROUPS and step < len(AV_STEPS):
                        if step == 0:
                            pe.wait_ge(pT_act.sem, pT_act.at(b, moves("A", 2 * G * (g + 1))))
                            pe.wait_ge(pT_dve.sem, pT_dve.at(b, moves("D", 2 * G * (g + 1))))
                        if step == 0 and g >= 1:
                            pe.wait_ge(o_norm.sem, o_norm.at(b, g))
                        for j in range(*AV_STEPS[step]):
                            for r in range(G):
                                u = G * g + r
                                h = u % H
                                nc.tensor.matmul(out_ps[HD * r:HD * (r + 1), :],
                                                 v_sb[:, j, h * HD:(h + 1) * HD], pT[:, u % PT_SLOTS, j, :],
                                                 start=j == 0, stop=j == NT - 1)
                    if 0 <= g < GROUPS and step == len(AV_STEPS) - 1:
                        pe.wait_ge(rinv_done.sem, rinv_done.at(b, g + 1))
                        for r in range(G):
                            u = G * g + r
                            last = nc.tensor.matmul(rinv_ps[HD * r:HD * (r + 1), :],
                                                    row_inv[:, u:u + 1].to_broadcast([P, HD]), ident,
                                                    start=True, stop=True)
                        last.then_inc(av.sem, 1)

                pe.wait_ge(logits.sem, logits.at(b, UNITS))
                for i in range(NP):
                    pe.wait_ge(o_norm.sem, o_norm.at(b, HG * (2 * i + 2)))
                    for t in (2 * i, 2 * i + 1):
                        for c in range(CT):
                            last = nc.tensor.matmul(bank[i][:, (t % 2) * D:(t % 2 + 1) * D],
                                                    oT[:, c, t * P:(t + 1) * P], wo[:, c, :],
                                                    start=c == 0, stop=c == CT - 1)
                    last.then_inc(y0_ps.sem, 1)
                    for k in range(3 + 2 * i, 5 + 2 * i if i < NP - 1 else NT * NH):
                        transpose_adj(k)

                def aggregate(dst, t, start, z_ready=None):
                    for j in range(NT):
                        if z_ready is not None:
                            pe.wait_ge(z_ready.sem, z_ready.at(b, j + 1))
                        rws = slice(t * P, (t + 1) * P)
                        last = split_product(dst, adjT_hi[:, j, rws], adjT_lo[:, j, rws], z_hi[:, j, :], z_lo[:, j, :],
                                             start and j == 0, j == NT - 1)
                    return last

                for half in range(NH):
                    pe.wait_ge(xn_done[0].sem, xn_done[0].at(b, TPH * (half + 1)))
                    rows_transposed(xn, half, 0, nT_ps[0])
                for t in range(NT):
                    if t % TPH == 0:
                        pe.wait_ge(nT_act[0].sem, nT_act[0].at(b, t // TPH + 1))
                        pe.wait_ge(nT_dve[0].sem, nT_dve[0].at(b, t // TPH + 1))
                    if t < 4:
                        pe.wait_ge(adjT_lo_done.sem, adjT_lo_done.at(b, NT * NH - 3 + t))
                    else:
                        pe.wait_ge(z_lo_done[0].sem, z_lo_done[0].at(b, t - 3))
                    for c in range(CT):
                        last = nc.tensor.matmul(late_bank(t), nT[:, c, t * P:(t + 1) * P],
                                                w_ns[:, c, :, :].rearrange("p a d -> p (a d)"),
                                                start=c == 0, stop=c == CT - 1)
                    last.then_inc(zs_ps.sem, 1)
                for t in range(NT):
                    if t >= 4:
                        pe.wait_ge(pre_done.sem, pre_done.at(b, t - 3))
                    if t == NT - 1:
                        pe.wait_ge(xn_done[1].sem, xn_done[1].at(b, TPH))
                        rows_transposed(xn, 0, 4, nT_ps[1])
                    aggregate(bank[t % 4][:, 0:D], t, True, z_lo_done[0] if t == 0 else None).then_inc(agg_ps.sem, 1)
                def root(i, t):
                    for c in range(CT):
                        nc.tensor.matmul(bank[4 + i][:, (t % 2) * D:(t % 2 + 1) * D], nT[:, c, t * P:(t + 1) * P],
                                         w_root[:, c, :], start=c == 0, stop=False)

                for half in range(NH):
                    if half == 1:
                        pe.wait_ge(xn_done[1].sem, xn_done[1].at(b, NT))
                        rows_transposed(xn, 1, 4, nT_ps[1])
                    else:
                        pe.wait_ge(pre_done.sem, pre_done.at(b, NT - 2))
                    pe.wait_ge(nT_act[1].sem, nT_act[1].at(b, half + 1))
                    pe.wait_ge(nT_dve[1].sem, nT_dve[1].at(b, half + 1))
                    for i in range(half * NP // NH, (half + 1) * NP // NH):
                        for t in (2 * i, 2 * i + 1):
                            for c in range(CT):
                                last = nc.tensor.matmul(bank[i][:, (t % 2) * D:(t % 2 + 1) * D],
                                                        nT[:, c, t * P:(t + 1) * P], w_rel[:, c, :],
                                                        start=c == 0, stop=c == CT - 1)
                        last.then_inc(z2_ps.sem, 1)
                    for i in range(half * NP // NH, (half + 1) * NP // NH):
                        root(i, 2 * i)
                pe.wait_ge(z_lo_done[1].sem, z_lo_done[1].at(b, NP))
                if has_next:
                    transpose_x(b + 1)
                for i in range(NP):
                    for t in (2 * i, 2 * i + 1):
                        dst = bank[4 + i][:, (t % 2) * D:(t % 2 + 1) * D]
                        if t % 2:
                            root(i, t)
                        last = aggregate(dst, t, False)
                    last.then_inc(conv_ps.sem, 1)
                if has_next:
                    pe.wait_ge(xT_act.sem, xT_act.at(b + 1, 2))
                    pe.wait_ge(xT_dve.sem, xT_dve.at(b + 1, 2))
                    for k in range(4):
                        project(b + 1, k, wq)
                    for k in range(4, 8):
                        pe.wait_ge(conv_b.sem, conv_b.at(b, k - 3))
                        project(b + 1, k, wk)
                    pe.wait_ge(qk_lo.sem, qk_lo.at(b + 1, 4))
                pe.wait_ge(x3_done.sem, x3_done.at(b, NT))
                pe.wait_ge(z_lo_done[2].sem, z_lo_done[2].at(b, NP))
                for k in range(CT * NH):
                    half, c = k // CT, k % CT
                    feats = slice(c * P, (c + 1) * P)
                    cols = slice(half * HALF, (half + 1) * HALF)
                    for j in range(NT):
                        split_product(bank[k][:, :], z_hi[:, j, feats], z_lo[:, j, feats], adjT_hi[:, j, cols],
                                      adjT_lo[:, j, cols], j == 0, False)
                    for i in range(TPH):
                        last = nc.tensor.matmul(bank[k][:, i * P:(i + 1) * P], cur[:, half * TPH + i, feats], diag_eps,
                                                start=False, stop=i == TPH - 1)
                    last.then_inc(h_ps.sem, 1)
                if has_next:
                    pe.wait_ge(qk_lo.sem, qk_lo.at(b + 1, 8))
                for k in range(KT * NH):
                    half, o = k // KT, k % KT
                    if o == 0:
                        pe.wait_ge(h_lo.sem, h_lo.at(b, CT * (half + 1)))
                    if k >= 4:
                        pe.wait_ge((u_act, u_dve)[k % 2].sem, (u_act, u_dve)[k % 2].at(b, (k - 4) // 2 + 1))
                    for c in range(CT):
                        outs, cols = slice(o * P, (o + 1) * P), slice(half * HALF, (half + 1) * HALF)
                        last = split_product(bank[4 + k % 4], w1_hi[:, c, outs], w1_lo[:, c, outs], hT_hi[:, c, cols],
                                             hT_lo[:, c, cols], c == 0, c == CT - 1)
                    last.then_inc(u_ps.sem, 1)
                for i in range(NP):
                    if i % (NP // NH) == 0:
                        half = i // (NP // NH)
                        pe.wait_ge(u_act.sem, u_act.at(b, (half + 1) * KT // 2))
                        pe.wait_ge(u_dve.sem, u_dve.at(b, (half + 1) * KT // 2))
                    for t in (2 * i, 2 * i + 1):
                        for c in range(KT):
                            last = nc.tensor.matmul(bank[i][:, (t % 2) * D:(t % 2 + 1) * D],
                                                    uT[:, c, t * P:(t + 1) * P], w2[:, c, :],
                                                    start=c == 0, stop=c == KT - 1)
                    last.then_inc(y3_ps.sem, 1)
                if has_next:
                    project_v(b + 1)

            pe.wait_ge(ident_done, 1)
            transpose_x(0)
            pe.wait_ge(projections_in, 3 * 16)
            pe.wait_ge(xT_act.sem, xT_act.at(0, 2))
            pe.wait_ge(xT_dve.sem, xT_dve.at(0, 2))
            for k in range(8):
                project(0, k, (wq, wk)[k // 4])
            pe.wait_ge(qk_lo.sem, qk_lo.at(0, 8))
            project_v(0)
            pe.wait_ge(consts, CONSTS)
            pe.wait_ge(weights_in, 16 * WEIGHT_DMAS)
            pe.wait_ge(w1_lo_done, 1)
            with pe.Fori(0, B - 1) as b:
                batch(b, True)
            batch(B - 1, False)


_INS = ["x", "adj", "L0_gnn_W_q", "L0_gnn_W_k", "L0_gnn_W_v", "L0_gnn_W_e", "L0_gnn_W_o", "L1_gnn_gamma",
        "L1_gnn_beta", "L1_gnn_W_self", "L1_gnn_W_neigh", "L2_gnn_W_rel", "L2_gnn_b_rel", "L2_gnn_W_root",
        "L2_gnn_ln_gamma", "L2_gnn_ln_beta", "L3_gnn_eps", "L3_gnn_W1", "L3_gnn_b1", "L3_gnn_W2", "L3_gnn_b2"]
_TRANSPOSED = ("L0_gnn_W_q", "L0_gnn_W_k", "L0_gnn_W_v", "L0_gnn_W_o")


def kernel(**inputs):
    import numpy as _np
    import concourse.bacc as _bacc
    from concourse import mybir as _mybir
    from concourse.bass_utils import run_bass_kernel_spmd as _run

    nc = _bacc.Bacc("TRN2", target_bir_lowering=False, num_devices=1)
    arrays, args = {}, []
    for name in _INS:
        a = _np.asarray(inputs[name])
        a = _np.ascontiguousarray(a.T if name in _TRANSPOSED else a)
        arrays[f"in_{name}_dram"] = a
        args.append(nc.dram_tensor(f"in_{name}_dram", a.shape, _mybir.dt.from_np(a.dtype), kind="ExternalInput").ap())
    shape = tuple(inputs["x"].shape)
    args.append(nc.dram_tensor("out_0_dram", shape, _mybir.dt.from_np(_np.dtype("float32")),
                               kind="ExternalOutput").ap())
    gnn_stack_kernel(nc, *args)
    r = _run(nc, [arrays], core_ids=[0])
    return r.results[0]["out_0_dram"]
```
